# Optimizing a Trainium2 kernel written in Bass

```python
import numpy as np
import jax
import jax.numpy as jnp

def _softmax(x, axis=-1):
    return jax.nn.softmax(x, axis=axis)

def _gelu(x):
    return jax.nn.gelu(x, approximate=True)

def _silu(x):
    return jax.nn.silu(x)

def _sigmoid(x):
    return jax.nn.sigmoid(x)

def _layernorm(x, axis=-1, eps=1e-05):
    m = jnp.mean(x, axis=axis, keepdims=True)
    v = jnp.var(x, axis=axis, keepdims=True)
    return (x - m) / jnp.sqrt(v + eps)

def _scatter_add(tgt, idx, src, axis=0):
    return tgt.at[idx].add(src)

def _segment_sum(src, seg, n):
    return jax.ops.segment_sum(src, seg, n)
kernel_name = 'mk_xattn_ffn_d1_seqx_r8_694b48'

def setup_inputs(seed: int=0):
    np.random.seed(seed)
    _w = jnp.asarray

    def _rec_inputs():
        import jax
        import jax.numpy as jnp
        _rk = jax.random.key(seed)
        x = -0.0002928 + 1 * jax.random.normal(jax.random.fold_in(_rk, 1), (8, 256, 128), jnp.float32)
        _lenS = 256 - jax.random.randint(jax.random.fold_in(_rk, 7), (8,), 0, max(1, 256 // 4) + 1, jnp.int32)
        _lenS2 = 512 - jax.random.randint(jax.random.fold_in(_rk, 8), (8,), 0, max(1, 512 // 4) + 1, jnp.int32)
        _ctx_2048P = jax.random.normal(jax.random.fold_in(_rk, 11), (8, 16, 256), jnp.float32)
        _ctx_2048c = jax.random.dirichlet(jax.random.fold_in(_rk, 511), 0.3 * jnp.ones((16,), jnp.float32), (8, 512))
        _ctx_2048t = jnp.einsum('bsk,bkd->bsd', _ctx_2048c, _ctx_2048P)
        _ctx_2048t = _ctx_2048t * jax.lax.rsqrt(jnp.mean(jnp.square(_ctx_2048t)) + 1e-12) * 0.953939
        ctx_2048 = -0.000514642 + 1.00011 * (_ctx_2048t + 0.3 * jax.random.normal(jax.random.fold_in(_rk, 611), (8, 512, 256), jnp.float32))
        return (x, ctx_2048)
    x, ctx_2048 = _rec_inputs()

    def _L0_xattn_setup():
        import jax, jax.numpy as jnp
        import numpy as np
        NUM_HEADS = 16
        key = jax.random.key(seed)
        ks = jax.random.split(key, 5)
        dim = 128
        B, N, N_c = (4, 128, 32)
        x = jax.random.normal(ks[0], (B, N, dim), dtype=jnp.float32)
        context = jax.random.normal(ks[1], (B, N_c, 2 * dim), dtype=jnp.float32)
        w_qkv = jax.random.normal(ks[2], (3 * dim, dim), dtype=jnp.float32) * 0.02
        w_proj = jax.random.normal(ks[3], (dim, dim), dtype=jnp.float32) * 0.02
        b_proj = jax.random.normal(ks[4], (dim,), dtype=jnp.float32) * 0.02
        return {'x': x, 'context': context, 'w_qkv': w_qkv, 'w_proj': w_proj, 'b_proj': b_proj}
    _L0_xattn_all = _L0_xattn_setup()
    _L0_xattn_in = {k: v for k, v in _L0_xattn_all.items() if k in ('w_qkv', 'w_proj', 'b_proj')}
    del _L0_xattn_all

    def _L0_ffn_setup():
        import jax, jax.numpy as jnp
        import numpy as np
        E, K = (8, 2)
        key = jax.random.key(seed)
        ks = jax.random.split(key, 5)
        B, S, H, I = (2, 128, 128, 512)
        scale_h = 1.0 / np.sqrt(H)
        scale_i = 1.0 / np.sqrt(I)
        return {'hidden_states': jax.random.normal(ks[0], (B, S, H), jnp.float32), 'conf_w': jax.random.normal(ks[1], (E, H), jnp.float32) * 0.1 * scale_h, 'conf_b': jnp.zeros((E,), jnp.float32), 'gate_w': jax.random.normal(ks[2], (E, I, H), jnp.float32) * scale_h, 'up_w': jax.random.normal(ks[3], (E, I, H), jnp.float32) * scale_h, 'down_w': jax.random.normal(ks[4], (E, H, I), jnp.float32) * scale_i, 'wealth': jnp.ones((E,), jnp.float32)}
    _L0_ffn_all = _L0_ffn_setup()
    _L0_ffn_in = {k: v for k, v in _L0_ffn_all.items() if k in ('conf_w', 'conf_b', 'gate_w', 'up_w', 'down_w', 'wealth')}
    del _L0_ffn_all
    return {'x': x, 'ctx_2048': ctx_2048, 'L0_xattn_w_qkv': _L0_xattn_in['w_qkv'], 'L0_xattn_w_proj': _L0_xattn_in['w_proj'], 'L0_xattn_b_proj': _L0_xattn_in['b_proj'], 'L0_ffn_conf_w': _L0_ffn_in['conf_w'], 'L0_ffn_conf_b': _L0_ffn_in['conf_b'], 'L0_ffn_gate_w': _L0_ffn_in['gate_w'], 'L0_ffn_up_w': _L0_ffn_in['up_w'], 'L0_ffn_down_w': _L0_ffn_in['down_w'], 'L0_ffn_wealth': _L0_ffn_in['wealth']}

def reference(x, ctx_2048, L0_xattn_w_qkv, L0_xattn_w_proj, L0_xattn_b_proj, L0_ffn_conf_w, L0_ffn_conf_b, L0_ffn_gate_w, L0_ffn_up_w, L0_ffn_down_w, L0_ffn_wealth):
    import jax
    import jax.numpy as jnp

    def _L0_xattn_ref(x, context, w_qkv, w_proj, b_proj):
        import jax, jax.numpy as jnp
        import numpy as np
        NUM_HEADS = 16
        B, N, C = x.shape
        H = NUM_HEADS
        D = C // H
        scale = D ** (-0.5)
        qkv = (x @ w_qkv.T).reshape(B, N, 3, H, D).transpose(2, 0, 3, 1, 4)
        q, k, v = (qkv[0], qkv[1], qkv[2])
        N_c = context.shape[1]
        kv = context.reshape(B, N_c, 2, H, D).transpose(2, 0, 3, 1, 4)
        extra_k, extra_v = (kv[0], kv[1])
        k = jnp.concatenate([extra_k, k], axis=2)
        v = jnp.concatenate([extra_v, v], axis=2)
        dtype = q.dtype
        attn = jnp.einsum('bhnd,bhmd->bhnm', q * scale, k).astype(jnp.float32)
        attn = jax.nn.softmax(attn, axis=-1).astype(dtype)
        out = jnp.einsum('bhnm,bhmd->bhnd', attn, v)
        out = out.transpose(0, 2, 1, 3).reshape(B, N, C)
        return out @ w_proj.T + b_proj

    def _L0_ffn_ref(hidden_states, conf_w, conf_b, gate_w, up_w, down_w, wealth):
        import jax, jax.numpy as jnp
        import numpy as np
        E, K = (8, 2)
        x = hidden_states
        confidences = jax.nn.sigmoid(jnp.einsum('bsh,eh->bse', x, conf_w) + conf_b)
        bids = confidences * wealth
        top_bids, selected_experts = jax.lax.top_k(bids, K)
        sorted_bids = -jnp.sort(-bids, axis=-1)
        payments = jnp.broadcast_to(sorted_bids[..., K:K + 1], top_bids.shape)
        routing_weights = jax.nn.softmax(top_bids, axis=-1)
        combine = jnp.sum(jax.nn.one_hot(selected_experts, E, dtype=x.dtype) * routing_weights[..., None], axis=2)

        def ffn(gw, uw, dw):
            g = jnp.einsum('bsh,ih->bsi', x, gw)
            u = jnp.einsum('bsh,ih->bsi', x, uw)
            return jnp.einsum('bsi,hi->bsh', jax.nn.silu(g) * u, dw)
        expert_out = jax.vmap(ffn)(gate_w, up_w, down_w)
        output = jnp.einsum('ebsh,bse->bsh', expert_out, combine)
        return output
    x = x + _L0_xattn_ref(_layernorm(x, axis=-1), ctx_2048, L0_xattn_w_qkv, L0_xattn_w_proj, L0_xattn_b_proj)
    x = x + _L0_ffn_ref(_layernorm(x, axis=-1), L0_ffn_conf_w, L0_ffn_conf_b, L0_ffn_gate_w, L0_ffn_up_w, L0_ffn_down_w, L0_ffn_wealth)
    return x

_drawn_inputs = setup_inputs


def setup_inputs(seed=0):
    import zlib

    import numpy as np

    out = dict(_drawn_inputs(seed))
    spreads = {'L0_ffn_conf_b': (0.0, 0.1), 'L0_ffn_wealth': (1.0, 0.2)}
    factors = {'L0_xattn_w_qkv': 5.619}
    for name, (base, spread) in spreads.items():
        noise = np.random.default_rng([zlib.crc32(name.encode()), seed]).standard_normal(out[name].shape)
        drawn = base * np.exp(spread * noise) if base else spread * noise
        out[name] = jnp.asarray(drawn.astype(out[name].dtype))
    for name, factor in factors.items():
        out[name] = (out[name] * factor).astype(out[name].dtype)
    return out
```

```python
from contextlib import ExitStack

import numpy as np

import concourse.bass as bass
from concourse import mybir

F32 = mybir.dt.float32
F32R = mybir.dt.float32r
I32 = mybir.dt.int32
ALU = mybir.AluOpType
ACT = mybir.ActivationFunctionType
AX = mybir.AxisListType

P = 128
B, N, C = 8, 256, 128
NC_ = 512
HEADS, D = 16, 8
QT = N // P
CT = NC_ // P
KT = CT + QT
KEYS = KT * P
TILES = B * QT
G = 4
T = HEADS // G
QUADS = B * T
ROWS = 32
SPLIT = 3 * D
SCALE = float(D) ** -0.5
EPS = 1e-5
E, I = 8, 512
IC = I // P
BANK = 512


def wait_for(engine, sem, value):
    if not isinstance(value, int) or value > 0:
        engine.wait_ge(sem, value)


def layernorm(vec, act, src, dst, stats, aggr, rstd, done):
    stats_in, aggr_in, std_in, rstd_in, norm_out = done

    def vector_stats():
        for i in range(TILES):
            vec.bn_stats(stats[:, i, :], src[:, i, :])\
               .then_inc(stats_in, 1)
        for i in range(TILES):
            vec.wait_ge(stats_in, i + 1)
            vec.bn_aggr(aggr[:, i, :], stats[:, i, :]).then_inc(aggr_in, 1)

    def scalar_std(eps):
        act.wait_ge(aggr_in, TILES)
        act.activation(rstd[:, 0, :], aggr[:, :, 1], ACT.Sqrt, bias=eps, scale=1.0).then_inc(std_in, 1)

    def vector_norm(i, first=False):
        if first:
            vec.wait_ge(std_in, 1)
            vec.reciprocal(rstd[:, 1, :], rstd[:, 0, :]).then_inc(rstd_in, 1)
            vec.wait_ge(rstd_in, 1)
        vec.tensor_scalar(dst[:, i, :], src[:, i, :], aggr[:, i, 0:1], rstd[:, 1, i:i + 1],
                          ALU.subtract, ALU.mult).then_inc(norm_out, 1)

    return vector_stats, scalar_std, vector_norm


def project(nc, m, d):
    with ExitStack() as ctx:
        sem = lambda name: ctx.enter_context(nc.semaphore(name))
        x_in, w_in = sem("x_in"), sem("w_in")
        ident_zero, ident_done, const_done = sem("ident_zero"), sem("ident_done"), sem("const_done")
        ln = [sem(n) for n in ("ln1_stats", "ln1_aggr", "ln1_std", "ln1_rstd", "ln1_norm")]
        xt_filled, xt_copied = sem("xt_filled"), sem("xt_copied")
        qkv_filled, qkv_copied = sem("qkv_filled"), sem("qkv_copied")
        bias_filled, bias_copied = sem("bias_filled"), sem("bias_copied")
        stats = ctx.enter_context(nc.sbuf_tensor("ln1_stats_sb", [P, TILES, 6], F32))
        aggr = ctx.enter_context(nc.sbuf_tensor("ln1_aggr_sb", [P, TILES, 2], F32))
        rstd = ctx.enter_context(nc.sbuf_tensor("ln1_rstd_sb", [P, 2, TILES], F32))
        xn = ctx.enter_context(nc.sbuf_tensor("xn", [P, TILES, C], F32))
        xnT = ctx.enter_context(nc.sbuf_tensor("xnT", [P, 2, P], F32))
        wqkv = ctx.enter_context(nc.sbuf_tensor("wqkv", [P, 3 * C], F32))
        xt_ps = [ctx.enter_context(nc.psum_tensor(f"xt_ps{i}", [P, BANK], F32)) for i in range(2)]
        qkv_ps = [ctx.enter_context(nc.psum_tensor(f"qkv_ps{i}", [P, BANK], F32)) for i in range(2)]
        block = ctx.enter_context(nc.Block())

        @block.sync
        def _(sp):
            sp.dma_start(m.x[:], d["x"].rearrange("b (t p) c -> p (b t) c", p=P)).then_inc(x_in, 16)
            sp.dma_start(wqkv[:], d["w_qkvT"]).then_inc(w_in, 16)
            sp.dma_start(m.wproj[:], d["w_projT"]).then_inc(w_in, 16)
            sp.dma_start(m.bproj[:], d["b_proj"].rearrange("(a c) -> a c", a=1)).then_inc(w_in, 16)
            for b in range(B):
                sp.dma_start(m.context[:, b * CT:(b + 1) * CT, :],
                             d["ctx"][b].rearrange("(t p) f -> p t f", p=P)).then_inc(m.context_in[b], 16)
            for w, src in ((m.gate, "gateT"), (m.up, "upT")):
                sp.dma_start(w[:], d[src].rearrange("e p i -> p e i")).then_inc(m.gate_up_in, 16)

        @block.gpsimd
        def _(pool):
            pool.memset(m.ident[:], 0.0).then_inc(ident_zero, 1)
            pool.memset(m.ones[:], 1.0).then_inc(const_done, 1)
            pool.memset(m.eps[:], EPS).then_inc(const_done, 1)
            pool.wait_ge(ident_zero, 1)
            pool.affine_select(out=m.ident[:], in_=m.ident[:], compare_op=ALU.not_equal, fill=1.0, base=0,
                               pattern=[[-1, P]], channel_multiplier=1).then_inc(ident_done, 1)
            pool.wait_ge(ident_done, 1)
            pool.tensor_copy(m.ident_r[:], m.ident[:]).then_inc(ident_done, 1)
            pool.memset(m.key_rows[:, :, :, :, SPLIT:SPLIT + 2].bitcast(F32), 1.0).then_inc(const_done, 1)
            pool.memset(m.key_rows[:, :, :, :, SPLIT + 2:ROWS].bitcast(F32), 0.0).then_inc(const_done, 1)
            pool.memset(m.query_rows[:, :, :, :, SPLIT:ROWS].bitcast(F32), 0.0).then_inc(const_done, 1)
            pool.memset(m.value_cols[:, :, :, :, D:D + 1], 1.0).then_inc(const_done, 1)
            pool.memset(m.value_cols[:, :, :, :, D + 1:ROWS], 0.0).then_inc(const_done, 1)

        @block.vector
        def _(vec):
            vector_stats, _, vector_norm = layernorm(vec, None, m.x, xn, stats, aggr, rstd, ln)
            vec.wait_ge(x_in, 16)
            vector_stats()
            vector_norm(0, first=True)
            vector_norm(1)
            vec.wait_ge(bias_filled, 1)
            vec.tensor_copy(m.bias[:], xt_ps[0][:, 0:C]).then_inc(bias_copied, 1)
            for i in range(TILES):
                if i + 2 < TILES:
                    vector_norm(i + 2)
                vec.wait_ge(xt_filled, i + 1)
                if i >= 2:
                    vec.wait_ge(qkv_filled, i - 1)
                vec.tensor_copy(xnT[:, i % 2, :], xt_ps[i % 2][:, 0:P]).then_inc(xt_copied, 1)
            vec.wait_ge(bias_copied, 1)
            vec.tensor_tensor(m.x[:], m.x[:], m.bias[:].unsqueeze(1).to_broadcast([P, TILES, C]), ALU.add)

        @block.scalar
        def _(act):
            _, scalar_std, _ = layernorm(None, act, m.x, xn, stats, aggr, rstd, ln)
            act.wait_ge(const_done, 2)
            scalar_std(m.eps[:])
            for i in range(TILES):
                act.wait_ge(qkv_filled, i + 1)
                act.activation(m.qkv[:, i, 0:C], qkv_ps[i % 2][:, 0:C], ACT.Copy, scale=SCALE)
                act.activation(m.qkv[:, i, C:3 * C], qkv_ps[i % 2][:, C:3 * C], ACT.Copy).then_inc(qkv_copied, 1)

        @block.tensor
        def _(pe):
            pe.wait_ge(w_in, 48)
            pe.wait_ge(const_done, 1)
            pe.matmul(xt_ps[0][:, 0:C], m.ones[0:1, :], m.bproj[0:1, :], start=True, stop=True).then_inc(bias_filled, 1)
            pe.wait_ge(ident_done, 1)
            for i in range(TILES + 1):
                if i < TILES:
                    pe.wait_ge(ln[4], i + 1)
                    if i == 0:
                        pe.wait_ge(bias_copied, 1)
                    if i >= 2:
                        pe.wait_ge(xt_copied, i - 1)
                    pe.transpose(xt_ps[i % 2][:, 0:P], xn[:, i, :], m.ident[:]).then_inc(xt_filled, 1)
                if i >= 1:
                    j = i - 1
                    pe.wait_ge(xt_copied, j + 1)
                    if j >= 2:
                        pe.wait_ge(qkv_copied, j - 1)
                    pe.matmul(qkv_ps[j % 2][:, 0:3 * C], xnT[:, j % 2, :], wqkv[:], start=True, stop=True)\
                      .then_inc(qkv_filled, 1)


UNIT_BANKS = 2
UNITS = KT
MAXES = 3 * G
EARLY = 3 * MAXES // 4
SHIFT_SLOT, OUT_SLOT, ATTN_SLOT, KEYS_SLOT, QUERIES_SLOT = 2, 3, 4, 4, 5
PV_SLOTS = [(), (0,), (1,), (2,), (3, 4), (5,)]


def attend(nc, m, d):
    with ExitStack() as ctx:
        sem = lambda name: ctx.enter_context(nc.semaphore(name))
        high_ready = sem("high_ready")
        rows_ready = sem("rows_ready")
        values_ready = sem("values_ready")
        keys_filled, keys_copied = sem("keys_filled"), sem("keys_copied")
        plain_copied = sem("plain_copied")
        max_filled, max_done = sem("max_filled"), sem("max_done")
        negmax_ready = sem("negmax_ready")
        shifted_filled, shifted_copied = sem("shifted_filled"), sem("shifted_copied")
        exp_filled, exp_done = sem("exp_filled"), sem("exp_done")
        pv_filled, pv_copied = sem("pv_filled"), sem("pv_copied")
        out_filled, out_done = sem("out_filled"), sem("out_done")
        attnT_filled, attnT_copied = sem("attnT_filled"), sem("attnT_copied")
        proj_filled, proj_done = sem("proj_filled"), sem("proj_done")
        blocks_zero = sem("blocks_zero")
        chain = sem("chain")
        rsum_ready = sem("rsum_ready")
        max_part = ctx.enter_context(nc.sbuf_tensor("max_part", [P, 2, G, 2, QT], F32))
        rowmax = ctx.enter_context(nc.sbuf_tensor("rowmax", [P, 2, G, QT], F32))
        plain = [ctx.enter_context(nc.sbuf_tensor(f"plain{i}", [P, G, N], F32R)) for i in range(2)]
        shifted = [ctx.enter_context(nc.sbuf_tensor(f"shifted{i}", [P, G, N], F32R)) for i in range(2)]
        probs = [ctx.enter_context(nc.sbuf_tensor(f"probs{i}", [P, KT, G, N], F32)) for i in range(2)]
        pv_sb = ctx.enter_context(nc.sbuf_tensor("pv_sb", [P, N], F32))
        rsum = ctx.enter_context(nc.sbuf_tensor("rsum", [P, 2, QT, G, 1], F32))
        attn = ctx.enter_context(nc.sbuf_tensor("attn", [P, QT, C], F32))
        attnT = ctx.enter_context(nc.sbuf_tensor("attnT", [P, QT, P], F32))
        exp_ps = [ctx.enter_context(nc.psum_tensor(f"exp_ps{i}", [P, UNIT_BANKS * BANK], F32)) for i in range(2)]
        max_ps = [ctx.enter_context(nc.psum_tensor(f"max_ps{i}", [P, BANK], F32)) for i in range(2)]
        pv_ps = ctx.enter_context(nc.psum_tensor("pv_ps", [P, BANK], F32))
        shared_ps = ctx.enter_context(nc.psum_tensor("shared_ps", [P, BANK], F32))
        shared_r = shared_ps[:].bitcast(F32R)
        block = ctx.enter_context(nc.Block())

        def steps(engine, step):
            for s in range(3):
                step(Step(0, s))
            with engine.Fori(0, B - 2) as b:
                for r in range(3, T + 3):
                    step(Step(b, r))
            for b in range(B - 2, B):
                for r in range(3, T + 3):
                    step(Step(b, r))

        class Step:

            def __init__(self, b, r):
                self.b, self.r, self.s = b, r, b * T + r
                inner = not isinstance(b, int)
                self.transposes = inner or self.s + 3 < QUADS
                self.early_maxes = inner or self.s + 2 < QUADS
                self.maxes = inner or self.s + 1 < QUADS
                self.scores = inner or self.s < QUADS
                self.product = inner or 1 <= self.s <= QUADS
                self.output = inner or 2 <= self.s < QUADS + 2
                self.transpose_out = r == T + 1
                self.project = r == T + 2

        @block.gpsimd
        def _(pool):
            heads = lambda ap: ap.rearrange("p k (g d) -> p k g d", d=D)

            def fill_rows(b, t, values):
                cols = lambda first: slice(first + G * D * t, first + G * D * (t + 1))
                ctx_k = heads(m.context[:, bass.ts(b, CT), cols(0)])
                own_k = heads(m.qkv[:, bass.ts(b, QT), cols(C)])
                own_q = heads(m.qkv[:, bass.ts(b, QT), cols(0)])
                kr, qr = m.key_rows[:, t], m.query_rows[:, t]
                for src, dst in ((ctx_k, kr[:, 0:CT]), (own_k, kr[:, CT:KT])):
                    pool.tensor_copy(dst[:, :, :, 0:D], src).then_inc(high_ready, 1)
                    pool.tensor_copy(dst[:, :, :, 2 * D:3 * D], src).then_inc(high_ready, 1)
                pool.tensor_copy(qr[:, :, :, 0:D], own_q).then_inc(high_ready, 1)
                pool.tensor_copy(qr[:, :, :, D:2 * D], own_q).then_inc(high_ready, 1)
                values()
                pool.tensor_tensor(kr[:, 0:CT, :, D:2 * D], ctx_k, kr[:, 0:CT, :, 0:D], ALU.subtract)\
                    .then_inc(rows_ready, 1)
                pool.tensor_tensor(kr[:, CT:KT, :, D:2 * D], own_k, kr[:, CT:KT, :, 0:D], ALU.subtract)\
                    .then_inc(rows_ready, 1)
                pool.tensor_tensor(qr[:, :, :, 2 * D:3 * D], own_q, qr[:, :, :, 0:D], ALU.subtract)\
                    .then_inc(rows_ready, 1)

            def fill_values(b, t):
                cols = lambda first: slice(first + G * D * t, first + G * D * (t + 1))
                pool.tensor_copy(m.value_cols[:, t, 0:CT, :, 0:D], heads(m.context[:, bass.ts(b, CT), cols(C)]))\
                    .then_inc(values_ready, 1)
                pool.tensor_copy(m.value_cols[:, t, CT:KT, :, 0:D], heads(m.qkv[:, bass.ts(b, QT), cols(2 * C)]))\
                    .then_inc(values_ready, 1)

            for half in plain + shifted:
                pool.memset(half[:].bitcast(F32), 0.0).then_inc(blocks_zero, 1)
            for b in range(B):
                pool.wait_ge(m.context_in[b], 16)
            def fill_quad(b, t):
                s = b * T + t

                def values():
                    if not (isinstance(b, int) and b == 0 and t == 0):
                        wait_for(pool, pv_filled, s - T)
                        pool.wait_ge(high_ready, s * 6 + 6)
                        fill_values(b if t else b - 1, (t - 1) % T)
                    else:
                        pool.wait_ge(high_ready, 6)
                fill_rows(b, t, values)

            for t in range(T):
                fill_quad(0, t)
            for t in range(T):
                pool.wait_ge(shifted_filled, t + 1)
                fill_quad(1, t)
            with pool.Fori(2, B) as b:
                for t in range(T):
                    pool.wait_ge(shifted_filled, b * T + (t - T + 1))
                    fill_quad(b, t)
            pool.wait_ge(pv_filled, QUADS - T)
            fill_values(B - 1, T - 1)

        @block.scalar
        def _(act):
            def copy_keys(s, t, half):
                act.wait_ge(keys_filled, s * 2 + (half + 1))
                cols = slice(half * BANK, min((half + 1) * BANK, KEYS))
                act.activation(m.keys[:, t, cols], shared_r[:, 0:cols.stop - cols.start], ACT.Copy)\
                   .then_inc(keys_copied, 1)
                for g in range(G if half else 0):
                    rows = slice(ROWS * g, ROWS * g + SPLIT)
                    act.activation(plain[t % 2][rows, g, :], shared_r[rows, N:2 * N], ACT.Copy)\
                       .then_inc(plain_copied, 1)

            def copy_shifted(s, parity):
                act.wait_ge(shifted_filled, s + 1)
                for g in range(G):
                    rows = slice(ROWS * g, ROWS * (g + 1))
                    act.activation(shifted[parity][rows, g, :], shared_r[rows, 0:N], ACT.Copy)\
                       .then_inc(shifted_copied, 1)

            def step(g):
                b, r, s = g.b, g.r, g.s
                for u in range(UNITS):
                    if u == SHIFT_SLOT and g.maxes:
                        copy_shifted(s + 1, (r + 1) % 2)
                    if u == ATTN_SLOT and g.transpose_out:
                        act.wait_ge(attnT_filled, b + 1)
                        act.activation(attnT[:], shared_ps[:, 0:QT * P].rearrange("p (q n) -> p q n", n=P), ACT.Copy)\
                           .then_inc(attnT_copied, 1)
                    if u == KEYS_SLOT and g.transposes:
                        copy_keys(s + 3, (r + 3) % T, 0)
                    if u == QUERIES_SLOT and g.transposes:
                        copy_keys(s + 3, (r + 3) % T, 1)
                    if g.scores:
                        if u == 0 and (g.output or r >= 2):
                            act.wait_ge(pv_filled, s - 1)
                        act.wait_ge(exp_filled, s * UNITS + (u + 1))
                        act.activation(probs[r % 2][:, u], exp_ps[u % 2][:].rearrange("p (g n) -> p g n", n=N),
                                       ACT.Exp).then_inc(exp_done, 1)
                    if u == 0 and g.output:
                        act.wait_ge(pv_filled, s - 1)
                        if r > 2:
                            act.wait_ge(out_filled, s - 2)
                        act.activation(pv_sb[:], pv_ps[:, 0:N], ACT.Copy).then_inc(pv_copied, 1)

            act.wait_ge(blocks_zero, 4)
            for q in range(2):
                copy_keys(q, q, 0)
                copy_keys(q, q, 1)
            copy_shifted(0, 0)
            copy_keys(2, 2, 0)
            copy_keys(2, 2, 1)
            steps(act, step)

        @block.vector
        def _(vec):
            def reduce_unit(s, w, par):
                g, part = divmod(w, 3)
                vec.wait_ge(max_filled, s * MAXES + (w + 1))
                if part < 2:
                    out, bank = max_part[:, par, g, 0, part:part + 1], max_ps[w % 2][:]
                else:
                    out, bank = max_part[:, par, g, 1, :], max_ps[w % 2][:].rearrange("p (q n) -> p q n", n=N)
                vec.reduce_max(out, bank, axis=AX.X).then_inc(max_done, 1)

            def negate_max(s, t, par):
                slot = lambda n: m.query_rows[:, t, :, :, n].rearrange("p q g -> p g q")
                vec.wait_ge(max_done, s * MAXES + MAXES)
                vec.tensor_tensor(rowmax[:, par], max_part[:, par, :, 0], max_part[:, par, :, 1], ALU.max)\
                   .then_inc(chain, 1)
                vec.wait_ge(chain, s * 2 + 1)
                vec.tensor_scalar(slot(SPLIT), rowmax[:, par], -1.0, None, ALU.mult).then_inc(chain, 1)
                vec.wait_ge(chain, s * 2 + 2)
                vec.scalar_tensor_tensor(slot(SPLIT + 1), rowmax[:, par], -1.0, slot(SPLIT), ALU.mult, ALU.subtract)\
                   .then_inc(negmax_ready, 1)

            def normalize(g):
                t, par = (g.r - 2) % T, g.r % 2
                quad_out = shared_ps[:, 0:QT * P].rearrange("p (q g k) -> p q g k", q=QT, g=G)
                vec.wait_ge(out_filled, g.s - 1)
                vec.reciprocal(rsum[:, par], quad_out[:, :, :, D:D + 1]).then_inc(rsum_ready, 1)
                vec.wait_ge(rsum_ready, g.s - 1)
                if g.project:
                    vec.wait_ge(attnT_filled, g.b + 1)
                vec.tensor_tensor(attn[:, :, G * D * t:G * D * (t + 1)].rearrange("p q (g k) -> p q g k", g=G),
                                  quad_out[:, :, :, 0:D], rsum[:, par].to_broadcast([P, QT, G, D]), ALU.mult)\
                   .then_inc(out_done, 1)

            def step(g):
                b, r, s = g.b, g.r, g.s
                if g.maxes:
                    reduce_unit(s + 1, EARLY, (r + 1) % 2)
                if g.project:
                    vec.wait_ge(proj_filled, b + 1)
                    vec.tensor_tensor(m.x[:, bass.ts(b, QT), :],
                                      shared_ps[:, 0:QT * C].rearrange("p (q c) -> p q c", c=C),
                                      m.x[:, bass.ts(b, QT), :], ALU.add).then_inc(proj_done, 1)
                if g.maxes:
                    for w in range(EARLY + 1, MAXES):
                        reduce_unit(s + 1, w, (r + 1) % 2)
                    negate_max(s + 1, (r + 1) % T, (r + 1) % 2)
                for w in range(EARLY):
                    if g.early_maxes:
                        reduce_unit(s + 2, w, r % 2)
                    if w == EARLY // 3 and g.output:
                        normalize(g)

            for w in range(MAXES):
                reduce_unit(0, w, 0)
            negate_max(0, 0, 0)
            for w in range(EARLY):
                reduce_unit(1, w, 1)
            steps(vec, step)

        @block.tensor
        def _(pe):
            def transpose_rows(s, t, half):
                if half == 0:
                    pe.wait_ge(rows_ready, s * 3 + 3)
                else:
                    pe.wait_ge(keys_copied, s * 2 + 1)
                for k in range(4 * half, 4 * half + 4):
                    tile = m.key_rows[:, t, k] if k < KT else m.query_rows[:, t, k - KT]
                    mm = pe.transpose(shared_r[:, (k % 4) * P:(k % 4 + 1) * P],
                                      tile.rearrange("p g k -> p (g k)"), m.ident_r[:])
                mm.then_inc(keys_filled, 1)

            def max_unit(s, w, t, wait=True):
                g, part = divmod(w, 3)
                if w == 0:
                    pe.wait_ge(keys_copied, s * 2 + 2)
                    pe.wait_ge(plain_copied, s * G + G)
                if wait:
                    pe.wait_ge(max_done, s * MAXES + (w - 1))
                if part < 2:
                    mm = pe.matmul(max_ps[w % 2][:], plain[t % 2][:, g, part * P:(part + 1) * P],
                                   m.keys[:, t, 0:NC_], start=True, stop=True)
                else:
                    for q in range(QT):
                        mm = pe.matmul(max_ps[w % 2][:, q * N:(q + 1) * N],
                                       plain[t % 2][:, g, q * P:(q + 1) * P], m.keys[:, t, NC_:KEYS],
                                       start=True, stop=True)
                mm.then_inc(max_filled, 1)

            def shift_rows(s, t):
                pe.wait_ge(negmax_ready, s + 1)
                for q in range(QT):
                    mm = pe.transpose(shared_r[:, q * P:(q + 1) * P],
                                      m.query_rows[:, t, q].rearrange("p g k -> p (g k)"), m.ident_r[:])
                mm.then_inc(shifted_filled, 1)

            def exp_unit(s, u, t, par, wait=True):
                if u == 0:
                    pe.wait_ge(shifted_copied, s * G + G)
                if wait:
                    pe.wait_ge(exp_done, s * UNITS + (u - 1))
                for half in range(UNIT_BANKS):
                    mm = pe.matmul(exp_ps[u % 2][:, half * BANK:(half + 1) * BANK], m.keys[:, t, u * P:(u + 1) * P],
                                   shifted[par][:, 2 * half:2 * half + 2, :], start=True, stop=True)
                mm.then_inc(exp_filled, 1)

            def pv_tile(s, k, t, par):
                if k == 0:
                    pe.wait_ge(exp_done, s * UNITS + UNITS)
                    pe.wait_ge(values_ready, s * 2 + 2)
                    pe.wait_ge(pv_copied, s)
                for g in range(G):
                    mm = pe.matmul(pv_ps[ROWS * g:ROWS * (g + 1), 0:N], m.value_cols[:, t, k, g, :],
                                   probs[par][:, k, g, :], start=(k == 0), stop=(k == KT - 1))
                if k == KT - 1:
                    mm.then_inc(pv_filled, 1)

            def step(g):
                b, r, s = g.b, g.r, g.s
                t, par = r % T, r % 2
                t1, t2 = (r + 1) % T, (r + 2) % T
                units = [(s + 1, w, t1) for w in range(EARLY, MAXES)] if g.maxes else []
                units += [(s + 2, w, t2) for w in range(EARLY)] if g.early_maxes else []

                def next_max():
                    if units:
                        max_unit(*units.pop(0))

                for u in range(UNITS):
                    next_max()
                    if u == 0 and g.project:
                        pe.wait_ge(attnT_copied, b + 1)
                        if g.early_maxes:
                            pe.wait_ge(plain_copied, s * G + 3 * G)
                        for q in range(QT):
                            mm = pe.matmul(shared_ps[:, q * C:(q + 1) * C], attnT[:, q, :], m.wproj[:],
                                           start=True, stop=True)
                        mm.then_inc(proj_filled, 1)
                    if u == SHIFT_SLOT and g.maxes:
                        if g.early_maxes:
                            pe.wait_ge(keys_copied, s * 2 + 6)
                            pe.wait_ge(plain_copied, s * G + 3 * G)
                        else:
                            pe.wait_ge(out_done, s - 2)
                        if g.project:
                            pe.wait_ge(proj_done, b + 1)
                        shift_rows(s + 1, t1)
                    if u == OUT_SLOT and g.output:
                        if g.maxes:
                            pe.wait_ge(shifted_copied, s * G + 2 * G)
                        else:
                            pe.wait_ge(out_done, s - 2)
                        pe.wait_ge(pv_copied, s - 1)
                        for q in range(QT):
                            mm = pe.transpose(shared_ps[:, q * P:(q + 1) * P], pv_sb[:, q * P:(q + 1) * P], m.ident[:])
                        mm.then_inc(out_filled, 1)
                    if u == ATTN_SLOT and g.transpose_out:
                        pe.wait_ge(out_done, s - 1)
                        for q in range(QT):
                            mm = pe.transpose(shared_ps[:, q * P:(q + 1) * P], attn[:, q, :], m.ident[:])
                        mm.then_inc(attnT_filled, 1)
                    if g.scores:
                        exp_unit(s, u, t, par, wait=r > 0 or u >= 2)
                    if u == KEYS_SLOT and g.transposes:
                        if g.output:
                            pe.wait_ge(out_done, s - 1)
                        else:
                            pe.wait_ge(shifted_copied, s * G + 2 * G)
                        if g.transpose_out:
                            pe.wait_ge(attnT_copied, b + 1)
                        transpose_rows(s + 3, (r + 3) % T, 0)
                    if u == QUERIES_SLOT and g.transposes:
                        transpose_rows(s + 3, (r + 3) % T, 1)
                    next_max()
                    if g.product:
                        for k in PV_SLOTS[u]:
                            pv_tile(s - 1, k, (r - 1) % T, 1 - par)

            transpose_rows(0, 0, 0)
            transpose_rows(0, 0, 1)
            for q in range(1, 2):
                pe.wait_ge(keys_copied, 2)
                pe.wait_ge(plain_copied, G)
                transpose_rows(q, q, 0)
                transpose_rows(q, q, 1)
            for w in range(MAXES):
                max_unit(0, w, 0, wait=w >= 2)
            pe.wait_ge(keys_copied, 4)
            pe.wait_ge(plain_copied, 2 * G)
            shift_rows(0, 0)
            pe.wait_ge(shifted_copied, G)
            transpose_rows(2, 2, 0)
            transpose_rows(2, 2, 1)
            for w in range(EARLY):
                max_unit(1, w, 1)
            steps(pe, step)


class Memory:

    def __init__(self, nc, ctx):
        sb = lambda name, shape, dt=F32: ctx.enter_context(nc.sbuf_tensor(name, shape, dt))
        self.x = sb("x", [P, TILES, C])
        self.context = sb("context", [P, B * CT, 2 * C])
        self.qkv = sb("qkv", [P, TILES, 3 * C])
        self.key_rows = sb("key_rows", [P, T, KT, G, ROWS], F32R)
        self.query_rows = sb("query_rows", [P, T, QT, G, ROWS], F32R)
        self.value_cols = sb("value_cols", [P, T, KT, G, ROWS])
        self.keys = sb("keys", [P, T, KEYS], F32R)
        self.wproj = sb("wproj", [P, C])
        self.bproj = sb("bproj", [1, C])
        self.bias = sb("bias", [P, C])
        self.ones = sb("ones", [P, P])
        self.eps = sb("eps_sb", [P, 1])
        self.ident = sb("ident", [P, P])
        self.ident_r = sb("ident_r", [P, P], F32R)
        self.gate, self.up = sb("gate", [P, E, I]), sb("up", [P, E, I])
        self.gate_up_in = ctx.enter_context(nc.semaphore("gate_up_in"))
        self.context_in = [ctx.enter_context(nc.semaphore(f"context_in{b}")) for b in range(B)]


def build(nc, d, out):
    with ExitStack() as ctx:
        m = Memory(nc, ctx)
        project(nc, m, d)
        attend(nc, m, d)
        experts(nc, m, d, out)


CHUNK = 4
CHUNKS = TILES // CHUNK


def experts(nc, m, d, out):
    with ExitStack() as ctx:
        sem = lambda name: ctx.enter_context(nc.semaphore(name))
        sb = lambda name, shape, dt=F32: ctx.enter_context(nc.sbuf_tensor(name, shape, dt))
        psum = lambda name: ctx.enter_context(nc.psum_tensor(name, [P, BANK], F32))
        ln = [sem(n) for n in ("ln2_stats", "ln2_aggr", "ln2_std", "ln2_rstd", "ln2_norm")]
        router_in, down_in, mask_zero, mask_ready = sem("router_in"), sem("down_in"), sem("mask_zero"), sem("mask_ready")
        ht_filled, ht_copied = sem("ht_filled"), sem("ht_copied")
        const_filled, const_copied = sem("const_filled"), sem("const_copied")
        logits_filled, logits_done, conf_done = sem("logits_filled"), sem("logits_done"), sem("conf_done")
        gap_ready, weights_done = sem("gap_ready"), sem("weights_done")
        route = sem("route")
        gate_filled, up_filled = sem("gate_filled"), sem("up_filled")
        silu_done, act_done = sem("silu_done"), sem("act_done")
        y_filled, y_done = sem("y_filled"), sem("y_done")
        stored = sem("stored")
        stats, aggr, rstd = sb("ln2_stats_sb", [P, TILES, 6]), sb("ln2_aggr_sb", [P, TILES, 2]), sb("ln2_rstd_sb", [P, 2, TILES])
        h = sb("h", [P, TILES, C])
        hT = sb("hT", [P, TILES * P])
        down = sb("down", [P, E, IC, C])
        conf_w = sb("conf_w", [P, E])
        conf_rows = sb("conf_rows", [1, 2 * E])
        conf_all = sb("conf_all", [P, 2, E])
        earlier = sb("earlier", [P, E, E])
        z, bids = sb("z", [P, TILES, E]), sb("bids", [P, TILES, E])
        pair, pair2 = sb("pair", [P, TILES, E, E]), sb("pair2", [P, TILES, E, E])
        rank = sb("rank", [P, TILES, E])
        top = sb("top", [P, 2, TILES, E])
        picked = sb("picked", [P, 2, TILES, E])
        best = sb("best", [P, 2, TILES, 1])
        gap, weight = sb("gap", [P, 2, TILES, 1]), sb("weight", [P, 2, TILES, 1])
        combine = sb("combine", [P, TILES, E])
        silu = sb("silu", [P, 2, BANK])
        act_T = sb("act_T", [P, 2, IC, BANK])
        t_ps = [psum(f"t_ps{i}") for i in range(2)]
        gate_ps, up_ps = [psum(f"gate_ps{i}") for i in range(2)], [psum(f"up_ps{i}") for i in range(2)]
        y_ps = [psum(f"y_ps{i}") for i in range(2)]
        block = ctx.enter_context(nc.Block())

        @block.sync
        def _(sp):
            sp.dma_start(conf_w[:], d["conf_wT"]).then_inc(router_in, 16)
            sp.dma_start(conf_rows[:, 0:E], d["conf_b"].rearrange("(a e) -> a e", a=1)).then_inc(router_in, 16)
            sp.dma_start(conf_rows[:, E:2 * E], d["wealth"].rearrange("(a e) -> a e", a=1)).then_inc(router_in, 16)
            sp.dma_start(down[:], d["downT"].rearrange("e (c p) h -> p e c h", p=P)).then_inc(down_in, 16)
            sp.wait_ge(y_done, CHUNKS * E * CHUNK)
            sp.dma_start(out.rearrange("b (t p) c -> p (b t) c", p=P), m.x[:]).then_inc(stored, 16)
            sp.wait_ge(stored, 16)

        @block.gpsimd
        def _(pool):
            pool.memset(earlier[:], 1.0).then_inc(mask_zero, 1)
            pool.wait_ge(mask_zero, 1)
            pool.affine_select(out=earlier[:], in_=earlier[:], compare_op=ALU.is_gt, fill=0.0, base=0,
                               pattern=[[1, E], [-1, E]], channel_multiplier=0).then_inc(mask_ready, 1)

        @block.scalar
        def _(act):
            _, scalar_std, _ = layernorm(None, act, m.x, h, stats, aggr, rstd, ln)
            scalar_std(m.eps[:])
            for k in range(CHUNKS):
                act.wait_ge(ht_filled, k + 1)
                act.activation(hT[:, k * BANK:(k + 1) * BANK], t_ps[k % 2][:], ACT.Copy).then_inc(ht_copied, 1)
            act.wait_ge(logits_done, 1)
            act.activation(bids[:], z[:], ACT.Sigmoid).then_inc(conf_done, 1)
            act.wait_ge(gap_ready, 2)
            act.activation(weight[:], gap[:], ACT.Sigmoid).then_inc(weights_done, 1)

            def chunk(c):
                for e in range(E):
                    for i in range(IC):
                        n = (c * E + e) * IC + i
                        act.wait_ge(gate_filled, n + 1)
                        wait_for(act, act_done, n - 1 if e * IC + i >= 2 else c * (E * IC))
                        act.activation(silu[:, i % 2, :], gate_ps[i % 2][:], ACT.Silu).then_inc(silu_done, 1)

            chunk(0)
            with act.Fori(1, CHUNKS) as c:
                chunk(c)

        @block.vector
        def _(vec):
            vector_stats, _, vector_norm = layernorm(vec, None, m.x, h, stats, aggr, rstd, ln)
            vector_stats()
            for i in range(TILES):
                vector_norm(i, first=i == 0)
            vec.wait_ge(const_filled, 1)
            vec.tensor_copy(conf_all[:], t_ps[0][:, 0:2 * E].rearrange("p (k e) -> p k e", e=E)).then_inc(const_copied, 1)
            vec.wait_ge(const_copied, 1)
            vec.wait_ge(logits_filled, 1)
            over_tiles = lambda ap: ap.unsqueeze(1).to_broadcast([P, TILES, E])
            vec.tensor_tensor(z[:], t_ps[1][:, 0:TILES * E].rearrange("p (t e) -> p t e", e=E),
                              over_tiles(conf_all[:, 0, :]), ALU.add).then_inc(logits_done, 1)
            steps = [0]

            def then(op):
                steps[0] += 1
                op.then_inc(route, 1)
                vec.wait_ge(route, steps[0])

            vec.wait_ge(conf_done, 1)
            then(vec.tensor_tensor(bids[:], bids[:], over_tiles(conf_all[:, 1, :]), ALU.mult))
            pairs = [P, TILES, E, E]
            this, other = bids[:].unsqueeze(3).to_broadcast(pairs), bids[:].unsqueeze(2).to_broadcast(pairs)
            vec.wait_ge(mask_ready, 1)
            then(vec.tensor_tensor(pair[:], other, this, ALU.is_equal))
            then(vec.tensor_tensor(pair[:], pair[:], earlier[:].unsqueeze(1).to_broadcast(pairs), ALU.mult))
            then(vec.tensor_tensor(pair2[:], other, this, ALU.is_gt))
            then(vec.tensor_tensor(pair[:], pair[:], pair2[:], ALU.add))
            then(vec.tensor_reduce(rank[:], pair[:], axis=AX.X, op=ALU.add))
            for k in range(2):
                then(vec.tensor_scalar(top[:, k], rank[:], float(k), None, ALU.is_equal))
                then(vec.tensor_tensor(picked[:, k], top[:, k], bids[:], ALU.mult))
                then(vec.tensor_reduce(best[:, k, :, 0], picked[:, k], axis=AX.X, op=ALU.add))
            for k in range(2):
                vec.tensor_tensor(gap[:, k], best[:, k], best[:, 1 - k], ALU.subtract).then_inc(gap_ready, 1)
            vec.wait_ge(weights_done, 1)
            for k in range(2):
                then(vec.tensor_tensor(picked[:, k], top[:, k], weight[:, k].to_broadcast([P, TILES, E]), ALU.mult))
            then(vec.tensor_tensor(combine[:], picked[:, 0], picked[:, 1], ALU.add))

            def product(n, i, act_buf, y_before):
                vec.wait_ge(silu_done, n + 1)
                vec.wait_ge(up_filled, n + 1)
                if i == 0:
                    wait_for(vec, y_filled, y_before)
                vec.tensor_tensor(act_T[:, act_buf, i, :], up_ps[i % 2][:], silu[:, i % 2, :], ALU.mult)\
                   .then_inc(act_done, 1)

            def add_y(tile0, n, e):
                vec.wait_ge(y_filled, n + 1)
                for k in range(CHUNK):
                    vec.scalar_tensor_tensor(m.x[:, bass.ds(tile0 + k, 1), :].rearrange("p a c -> p (a c)"),
                                             y_ps[e % 2][:, k * C:(k + 1) * C],
                                             combine[:, bass.ds(tile0 + k, 1), e:e + 1].rearrange("p a c -> p (a c)"),
                                             m.x[:, bass.ds(tile0 + k, 1), :].rearrange("p a c -> p (a c)"),
                                             ALU.mult, ALU.add).then_inc(y_done, 1)

            def chunk(c):
                for e in range(E):
                    n = c * E + e
                    for i in range(IC):
                        product(n * IC + i, i, e % 2, n - 1 if e else c * E)
                    if e:
                        wait_for(vec, y_done, (n - 1) * CHUNK)
                        add_y(c * CHUNK, n - 1, e - 1)
                vec.wait_ge(y_done, (c * E + (E - 1)) * CHUNK)
                add_y(c * CHUNK, c * E + (E - 1), E - 1)

            chunk(0)
            with vec.Fori(1, CHUNKS) as c:
                chunk(c)

        @block.tensor
        def _(pe):
            for k in range(CHUNKS):
                pe.wait_ge(ln[4], (k + 1) * CHUNK)
                if k >= 2:
                    pe.wait_ge(ht_copied, k - 1)
                for i in range(CHUNK):
                    mm = pe.transpose(t_ps[k % 2][:, i * P:(i + 1) * P], h[:, k * CHUNK + i, :], m.ident[:])
                mm.then_inc(ht_filled, 1)
            pe.wait_ge(ht_copied, CHUNKS)
            pe.wait_ge(router_in, 48)
            pe.matmul(t_ps[0][:, 0:2 * E], m.ones[0:1, :], conf_rows[0:1, :], start=True, stop=True)\
              .then_inc(const_filled, 1)
            for i in range(TILES):
                mm = pe.matmul(t_ps[1][:, i * E:(i + 1) * E], hT[:, i * P:(i + 1) * P], conf_w[:], start=True, stop=True)
            mm.then_inc(logits_filled, 1)
            pe.wait_ge(m.gate_up_in, 32)
            pe.wait_ge(down_in, 16)

            def hidden(c, e):
                n0 = (c * E + e) * IC
                for i in range(IC):
                    for w, ps, filled, used in ((m.gate, gate_ps, gate_filled, silu_done), (m.up, up_ps, up_filled, act_done)):
                        wait_for(pe, used, n0 + (i - 1) if e * IC + i >= 2 else c * (E * IC))
                        pe.matmul(ps[i % 2][:], w[:, e, i * P:(i + 1) * P], hT[:, bass.ts(c, BANK)], start=True, stop=True)\
                          .then_inc(filled, 1)

            def output(c, e):
                n = c * E + e
                pe.wait_ge(act_done, n * IC + IC)
                wait_for(pe, y_done, (n - 1) * CHUNK if e >= 2 else c * (E * CHUNK))
                for k in range(CHUNK):
                    for i in range(IC):
                        mm = pe.matmul(y_ps[e % 2][:, k * C:(k + 1) * C], act_T[:, e % 2, i, k * P:(k + 1) * P],
                                       down[:, e, i, :], start=(i == 0), stop=(i == IC - 1))
                mm.then_inc(y_filled, 1)

            def chunk(c):
                for e in range(E):
                    hidden(c, e)
                    if e:
                        output(c, e - 1)
                output(c, E - 1)

            chunk(0)
            with pe.Fori(1, CHUNKS) as c:
                chunk(c)


def kernel(x, ctx_2048, L0_xattn_w_qkv, L0_xattn_w_proj, L0_xattn_b_proj, L0_ffn_conf_w, L0_ffn_conf_b,
           L0_ffn_gate_w, L0_ffn_up_w, L0_ffn_down_w, L0_ffn_wealth):
    import concourse.bacc as bacc
    from concourse.bass_utils import run_bass_kernel_spmd

    t = lambda a: np.ascontiguousarray(np.swapaxes(np.asarray(a), -1, -2))
    arrays = {
        "x": np.asarray(x), "ctx": np.asarray(ctx_2048), "w_qkvT": t(L0_xattn_w_qkv),
        "w_projT": t(L0_xattn_w_proj), "b_proj": np.asarray(L0_xattn_b_proj),
        "conf_wT": t(L0_ffn_conf_w), "conf_b": np.asarray(L0_ffn_conf_b), "wealth": np.asarray(L0_ffn_wealth),
        "gateT": t(L0_ffn_gate_w), "upT": t(L0_ffn_up_w), "downT": t(L0_ffn_down_w),
    }
    nc = bacc.Bacc("TRN2", target_bir_lowering=False, num_devices=1)
    d = {k: nc.dram_tensor(f"{k}_dram", a.shape, mybir.dt.from_np(a.dtype), kind="ExternalInput").ap() for k, a in arrays.items()}
    out = nc.dram_tensor("out_dram", (B, N, C), F32, kind="ExternalOutput").ap()
    build(nc, d, out)
    r = run_bass_kernel_spmd(nc, [{f"{k}_dram": a for k, a in arrays.items()}], core_ids=[0])
    return r.results[0]["out_dram"]
```

```python
from contextlib import ExitStack

import numpy as np

import concourse.bass as bass
from concourse import mybir

F32 = mybir.dt.float32
F32R = mybir.dt.float32r
I32 = mybir.dt.int32
ALU = mybir.AluOpType
ACT = mybir.ActivationFunctionType
AX = mybir.AxisListType

P = 128
B, N, C = 8, 256, 128
NC_ = 512
HEADS, D = 16, 8
QT = N // P
CT = NC_ // P
KT = CT + QT
KEYS = KT * P
TILES = B * QT
G = 4
T = HEADS // G
QUADS = B * T
ROWS = 32
SPLIT = 3 * D
SCALE = float(D) ** -0.5
EPS = 1e-5
E, I = 8, 512
IC = I // P
BANK = 512


def wait_for(engine, sem, value):
    if not isinstance(value, int) or value > 0:
        engine.wait_ge(sem, value)


def layernorm(vec, act, src, dst, stats, aggr, rstd, done):
    stats_in, aggr_in, std_in, rstd_in, norm_out = done

    def vector_stats():
        for i in range(TILES):
            vec.bn_stats(stats[:, i, :], src[:, i, :])\
               .then_inc(stats_in, 1)
        for i in range(TILES):
            vec.wait_ge(stats_in, i + 1)
            vec.bn_aggr(aggr[:, i, :], stats[:, i, :]).then_inc(aggr_in, 1)

    def scalar_std(eps):
        act.wait_ge(aggr_in, TILES)
        act.activation(rstd[:, 0, :], aggr[:, :, 1], ACT.Sqrt, bias=eps, scale=1.0).then_inc(std_in, 1)

    def vector_norm(i, first=False):
        if first:
            vec.wait_ge(std_in, 1)
            vec.reciprocal(rstd[:, 1, :], rstd[:, 0, :]).then_inc(rstd_in, 1)
            vec.wait_ge(rstd_in, 1)
        vec.tensor_scalar(dst[:, i, :], src[:, i, :], aggr[:, i, 0:1], rstd[:, 1, i:i + 1],
                          ALU.subtract, ALU.mult).then_inc(norm_out, 1)

    return vector_stats, scalar_std, vector_norm


def project(nc, m, d):
    with ExitStack() as ctx:
        sem = lambda name: ctx.enter_context(nc.semaphore(name))
        x_in, w_in = sem("x_in"), sem("w_in")
        ident_zero, ident_done, const_done = sem("ident_zero"), sem("ident_done"), sem("const_done")
        ln = [sem(n) for n in ("ln1_stats", "ln1_aggr", "ln1_std", "ln1_rstd", "ln1_norm")]
        xt_filled, xt_copied = sem("xt_filled"), sem("xt_copied")
        qkv_filled, qkv_copied = sem("qkv_filled"), sem("qkv_copied")
        bias_filled, bias_copied = sem("bias_filled"), sem("bias_copied")
        stats = ctx.enter_context(nc.sbuf_tensor("ln1_stats_sb", [P, TILES, 6], F32))
        aggr = ctx.enter_context(nc.sbuf_tensor("ln1_aggr_sb", [P, TILES, 2], F32))
        rstd = ctx.enter_context(nc.sbuf_tensor("ln1_rstd_sb", [P, 2, TILES], F32))
        xn = ctx.enter_context(nc.sbuf_tensor("xn", [P, TILES, C], F32))
        xnT = ctx.enter_context(nc.sbuf_tensor("xnT", [P, 2, P], F32))
        wqkv = ctx.enter_context(nc.sbuf_tensor("wqkv", [P, 3 * C], F32))
        xt_ps = [ctx.enter_context(nc.psum_tensor(f"xt_ps{i}", [P, BANK], F32)) for i in range(2)]
        qkv_ps = [ctx.enter_context(nc.psum_tensor(f"qkv_ps{i}", [P, BANK], F32)) for i in range(2)]
        block = ctx.enter_context(nc.Block())

        @block.sync
        def _(sp):
            sp.dma_start(m.x[:], d["x"].rearrange("b (t p) c -> p (b t) c", p=P)).then_inc(x_in, 16)
            sp.dma_start(wqkv[:], d["w_qkvT"]).then_inc(w_in, 16)
            sp.dma_start(m.wproj[:], d["w_projT"]).then_inc(w_in, 16)
            sp.dma_start(m.bproj[:], d["b_proj"].rearrange("(a c) -> a c", a=1)).then_inc(w_in, 16)
            for b in range(B):
                sp.dma_start(m.context[:, b * CT:(b + 1) * CT, :],
                             d["ctx"][b].rearrange("(t p) f -> p t f", p=P)).then_inc(m.context_in[b], 16)
            for w, src in ((m.gate, "gateT"), (m.up, "upT")):
                sp.dma_start(w[:], d[src].rearrange("e p i -> p e i")).then_inc(m.gate_up_in, 16)

        @block.gpsimd
        def _(pool):
            pool.memset(m.ident[:], 0.0).then_inc(ident_zero, 1)
            pool.memset(m.ones[:], 1.0).then_inc(const_done, 1)
            pool.memset(m.eps[:], EPS).then_inc(const_done, 1)
            pool.wait_ge(ident_zero, 1)
            pool.affine_select(out=m.ident[:], in_=m.ident[:], compare_op=ALU.not_equal, fill=1.0, base=0,
                               pattern=[[-1, P]], channel_multiplier=1).then_inc(ident_done, 1)
            pool.wait_ge(ident_done, 1)
            pool.tensor_copy(m.ident_r[:], m.ident[:]).then_inc(ident_done, 1)
            pool.memset(m.key_rows[:, :, :, :, SPLIT:SPLIT + 2].bitcast(F32), 1.0).then_inc(const_done, 1)
            pool.memset(m.key_rows[:, :, :, :, SPLIT + 2:ROWS].bitcast(F32), 0.0).then_inc(const_done, 1)
            pool.memset(m.query_rows[:, :, :, :, SPLIT:ROWS].bitcast(F32), 0.0).then_inc(const_done, 1)
            pool.memset(m.value_cols[:, :, :, :, D:D + 1], 1.0).then_inc(const_done, 1)
            pool.memset(m.value_cols[:, :, :, :, D + 1:ROWS], 0.0).then_inc(const_done, 1)

        @block.vector
        def _(vec):
            vector_stats, _, vector_norm = layernorm(vec, None, m.x, xn, stats, aggr, rstd, ln)
            vec.wait_ge(x_in, 16)
            vector_stats()
            vector_norm(0, first=True)
            vector_norm(1)
            vec.wait_ge(bias_filled, 1)
            vec.tensor_copy(m.bias[:], xt_ps[0][:, 0:C]).then_inc(bias_copied, 1)
            for i in range(TILES):
                if i + 2 < TILES:
                    vector_norm(i + 2)
                vec.wait_ge(xt_filled, i + 1)
                if i >= 2:
                    vec.wait_ge(qkv_filled, i - 1)
                vec.tensor_copy(xnT[:, i % 2, :], xt_ps[i % 2][:, 0:P]).then_inc(xt_copied, 1)
            vec.wait_ge(bias_copied, 1)
            vec.tensor_tensor(m.x[:], m.x[:], m.bias[:].unsqueeze(1).to_broadcast([P, TILES, C]), ALU.add)

        @block.scalar
        def _(act):
            _, scalar_std, _ = layernorm(None, act, m.x, xn, stats, aggr, rstd, ln)
            act.wait_ge(const_done, 2)
            scalar_std(m.eps[:])
            for i in range(TILES):
                act.wait_ge(qkv_filled, i + 1)
                act.activation(m.qkv[:, i, 0:C], qkv_ps[i % 2][:, 0:C], ACT.Copy, scale=SCALE)
                act.activation(m.qkv[:, i, C:3 * C], qkv_ps[i % 2][:, C:3 * C], ACT.Copy).then_inc(qkv_copied, 1)

        @block.tensor
        def _(pe):
            pe.wait_ge(w_in, 48)
            pe.wait_ge(const_done, 1)
            pe.matmul(xt_ps[0][:, 0:C], m.ones[0:1, :], m.bproj[0:1, :], start=True, stop=True).then_inc(bias_filled, 1)
            pe.wait_ge(ident_done, 1)
            for i in range(TILES + 1):
                if i < TILES:
                    pe.wait_ge(ln[4], i + 1)
                    if i == 0:
                        pe.wait_ge(bias_copied, 1)
                    if i >= 2:
                        pe.wait_ge(xt_copied, i - 1)
                    pe.transpose(xt_ps[i % 2][:, 0:P], xn[:, i, :], m.ident[:]).then_inc(xt_filled, 1)
                if i >= 1:
                    j = i - 1
                    pe.wait_ge(xt_copied, j + 1)
                    if j >= 2:
                        pe.wait_ge(qkv_copied, j - 1)
                    pe.matmul(qkv_ps[j % 2][:, 0:3 * C], xnT[:, j % 2, :], wqkv[:], start=True, stop=True)\
                      .then_inc(qkv_filled, 1)


UNIT_BANKS = 2
UNITS = KT
MAXES = 3 * G
EARLY = 3 * MAXES // 4
SHIFT_SLOT, OUT_SLOT, ATTN_SLOT, KEYS_SLOT, QUERIES_SLOT = 2, 3, 4, 4, 5
PV_SLOTS = [(), (0,), (1,), (2,), (3, 4), (5,)]


def attend(nc, m, d):
    with ExitStack() as ctx:
        sem = lambda name: ctx.enter_context(nc.semaphore(name))
        high_ready = sem("high_ready")
        rows_ready = sem("rows_ready")
        values_ready = sem("values_ready")
        keys_filled, keys_copied = sem("keys_filled"), sem("keys_copied")
        plain_copied = sem("plain_copied")
        max_filled, max_done = sem("max_filled"), sem("max_done")
        negmax_ready = sem("negmax_ready")
        shifted_filled, shifted_copied = sem("shifted_filled"), sem("shifted_copied")
        exp_filled, exp_done = sem("exp_filled"), sem("exp_done")
        pv_filled, pv_copied = sem("pv_filled"), sem("pv_copied")
        out_filled, out_done = sem("out_filled"), sem("out_done")
        attnT_filled, attnT_copied = sem("attnT_filled"), sem("attnT_copied")
        proj_filled, proj_done = sem("proj_filled"), sem("proj_done")
        blocks_zero = sem("blocks_zero")
        chain = sem("chain")
        rsum_ready = sem("rsum_ready")
        max_part = ctx.enter_context(nc.sbuf_tensor("max_part", [P, 2, G, 2, QT], F32))
        rowmax = ctx.enter_context(nc.sbuf_tensor("rowmax", [P, 2, G, QT], F32))
        plain = [ctx.enter_context(nc.sbuf_tensor(f"plain{i}", [P, G, N], F32R)) for i in range(2)]
        shifted = [ctx.enter_context(nc.sbuf_tensor(f"shifted{i}", [P, G, N], F32R)) for i in range(2)]
        probs = [ctx.enter_context(nc.sbuf_tensor(f"probs{i}", [P, KT, G, N], F32)) for i in range(2)]
        pv_sb = ctx.enter_context(nc.sbuf_tensor("pv_sb", [P, N], F32))
        rsum = ctx.enter_context(nc.sbuf_tensor("rsum", [P, 2, QT, G, 1], F32))
        attn = ctx.enter_context(nc.sbuf_tensor("attn", [P, QT, C], F32))
        attnT = ctx.enter_context(nc.sbuf_tensor("attnT", [P, QT, P], F32))
        exp_ps = [ctx.enter_context(nc.psum_tensor(f"exp_ps{i}", [P, UNIT_BANKS * BANK], F32)) for i in range(2)]
        max_ps = [ctx.enter_context(nc.psum_tensor(f"max_ps{i}", [P, BANK], F32)) for i in range(2)]
        pv_ps = ctx.enter_context(nc.psum_tensor("pv_ps", [P, BANK], F32))
        shared_ps = ctx.enter_context(nc.psum_tensor("shared_ps", [P, BANK], F32))
        shared_r = shared_ps[:].bitcast(F32R)
        block = ctx.enter_context(nc.Block())

        def steps(engine, step):
            for s in range(3):
                step(Step(0, s))
            with engine.Fori(0, B - 2) as b:
                for r in range(3, T + 3):
                    step(Step(b, r))
            for b in range(B - 2, B):
                for r in range(3, T + 3):
                    step(Step(b, r))

        class Step:

            def __init__(self, b, r):
                self.b, self.r, self.s = b, r, b * T + r
                inner = not isinstance(b, int)
                self.transposes = inner or self.s + 3 < QUADS
                self.early_maxes = inner or self.s + 2 < QUADS
                self.maxes = inner or self.s + 1 < QUADS
                self.scores = inner or self.s < QUADS
                self.product = inner or 1 <= self.s <= QUADS
                self.output = inner or 2 <= self.s < QUADS + 2
                self.transpose_out = r == T + 1
                self.project = r == T + 2

        @block.gpsimd
        def _(pool):
            heads = lambda ap: ap.rearrange("p k (g d) -> p k g d", d=D)

            def fill_rows(b, t, values):
                cols = lambda first: slice(first + G * D * t, first + G * D * (t + 1))
                ctx_k = heads(m.context[:, bass.ts(b, CT), cols(0)])
                own_k = heads(m.qkv[:, bass.ts(b, QT), cols(C)])
                own_q = heads(m.qkv[:, bass.ts(b, QT), cols(0)])
                kr, qr = m.key_rows[:, t], m.query_rows[:, t]
                for src, dst in ((ctx_k, kr[:, 0:CT]), (own_k, kr[:, CT:KT])):
                    pool.tensor_copy(dst[:, :, :, 0:D], src).then_inc(high_ready, 1)
                    pool.tensor_copy(dst[:, :, :, 2 * D:3 * D], src).then_inc(high_ready, 1)
                pool.tensor_copy(qr[:, :, :, 0:D], own_q).then_inc(high_ready, 1)
                pool.tensor_copy(qr[:, :, :, D:2 * D], own_q).then_inc(high_ready, 1)
                values()
                pool.tensor_tensor(kr[:, 0:CT, :, D:2 * D], ctx_k, kr[:, 0:CT, :, 0:D], ALU.subtract)\
                    .then_inc(rows_ready, 1)
                pool.tensor_tensor(kr[:, CT:KT, :, D:2 * D], own_k, kr[:, CT:KT, :, 0:D], ALU.subtract)\
                    .then_inc(rows_ready, 1)
                pool.tensor_tensor(qr[:, :, :, 2 * D:3 * D], own_q, qr[:, :, :, 0:D], ALU.subtract)\
                    .then_inc(rows_ready, 1)

            def fill_values(b, t):
                cols = lambda first: slice(first + G * D * t, first + G * D * (t + 1))
                pool.tensor_copy(m.value_cols[:, t, 0:CT, :, 0:D], heads(m.context[:, bass.ts(b, CT), cols(C)]))\
                    .then_inc(values_ready, 1)
                pool.tensor_copy(m.value_cols[:, t, CT:KT, :, 0:D], heads(m.qkv[:, bass.ts(b, QT), cols(2 * C)]))\
                    .then_inc(values_ready, 1)

            for half in plain + shifted:
                pool.memset(half[:].bitcast(F32), 0.0).then_inc(blocks_zero, 1)
            for b in range(B):
                pool.wait_ge(m.context_in[b], 16)
            def fill_quad(b, t):
                s = b * T + t

                def values():
                    if not (isinstance(b, int) and b == 0 and t == 0):
                        wait_for(pool, pv_filled, s - T)
                        pool.wait_ge(high_ready, s * 6 + 6)
                        fill_values(b if t else b - 1, (t - 1) % T)
                    else:
                        pool.wait_ge(high_ready, 6)
                fill_rows(b, t, values)

            for t in range(T):
                fill_quad(0, t)
            for t in range(T):
                pool.wait_ge(shifted_filled, t + 1)
                fill_quad(1, t)
            with pool.Fori(2, B) as b:
                for t in range(T):
                    pool.wait_ge(shifted_filled, b * T + (t - T + 1))
                    fill_quad(b, t)
            pool.wait_ge(pv_filled, QUADS - T)
            fill_values(B - 1, T - 1)

        @block.scalar
        def _(act):
            def copy_keys(s, t, half):
                act.wait_ge(keys_filled, s * 2 + (half + 1))
                cols = slice(half * BANK, min((half + 1) * BANK, KEYS))
                act.activation(m.keys[:, t, cols], shared_r[:, 0:cols.stop - cols.start], ACT.Copy)\
                   .then_inc(keys_copied, 1)
                for g in range(G if half else 0):
                    rows = slice(ROWS * g, ROWS * g + SPLIT)
                    act.activation(plain[t % 2][rows, g, :], shared_r[rows, N:2 * N], ACT.Copy)\
                       .then_inc(plain_copied, 1)

            def copy_shifted(s, parity):
                act.wait_ge(shifted_filled, s + 1)
                for g in range(G):
                    rows = slice(ROWS * g, ROWS * (g + 1))
                    act.activation(shifted[parity][rows, g, :], shared_r[rows, 0:N], ACT.Copy)\
                       .then_inc(shifted_copied, 1)

            def step(g):
                b, r, s = g.b, g.r, g.s
                for u in range(UNITS):
                    if u == SHIFT_SLOT and g.maxes:
                        copy_shifted(s + 1, (r + 1) % 2)
                    if u == ATTN_SLOT and g.transpose_out:
                        act.wait_ge(attnT_filled, b + 1)
                        act.activation(attnT[:], shared_ps[:, 0:QT * P].rearrange("p (q n) -> p q n", n=P), ACT.Copy)\
                           .then_inc(attnT_copied, 1)
                    if u == KEYS_SLOT and g.transposes:
                        copy_keys(s + 3, (r + 3) % T, 0)
                    if u == QUERIES_SLOT and g.transposes:
                        copy_keys(s + 3, (r + 3) % T, 1)
                    if g.scores:
                        if u == 0 and (g.output or r >= 2):
                            act.wait_ge(pv_filled, s - 1)
                        act.wait_ge(exp_filled, s * UNITS + (u + 1))
                        act.activation(probs[r % 2][:, u], exp_ps[u % 2][:].rearrange("p (g n) -> p g n", n=N),
                                       ACT.Exp).then_inc(exp_done, 1)
                    if u == 0 and g.output:
                        act.wait_ge(pv_filled, s - 1)
                        if r > 2:
                            act.wait_ge(out_filled, s - 2)
                        act.activation(pv_sb[:], pv_ps[:, 0:N], ACT.Copy).then_inc(pv_copied, 1)

            act.wait_ge(blocks_zero, 4)
            for q in range(2):
                copy_keys(q, q, 0)
                copy_keys(q, q, 1)
            copy_shifted(0, 0)
            copy_keys(2, 2, 0)
            copy_keys(2, 2, 1)
            steps(act, step)

        @block.vector
        def _(vec):
            def reduce_unit(s, w, par):
                g, part = divmod(w, 3)
                vec.wait_ge(max_filled, s * MAXES + (w + 1))
                if part < 2:
                    out, bank = max_part[:, par, g, 0, part:part + 1], max_ps[w % 2][:]
                else:
                    out, bank = max_part[:, par, g, 1, :], max_ps[w % 2][:].rearrange("p (q n) -> p q n", n=N)
                vec.reduce_max(out, bank, axis=AX.X).then_inc(max_done, 1)

            def negate_max(s, t, par):
                slot = lambda n: m.query_rows[:, t, :, :, n].rearrange("p q g -> p g q")
                vec.wait_ge(max_done, s * MAXES + MAXES)
                vec.tensor_tensor(rowmax[:, par], max_part[:, par, :, 0], max_part[:, par, :, 1], ALU.max)\
                   .then_inc(chain, 1)
                vec.wait_ge(chain, s * 2 + 1)
                vec.tensor_scalar(slot(SPLIT), rowmax[:, par], -1.0, None, ALU.mult).then_inc(chain, 1)
                vec.wait_ge(chain, s * 2 + 2)
                vec.scalar_tensor_tensor(slot(SPLIT + 1), rowmax[:, par], -1.0, slot(SPLIT), ALU.mult, ALU.subtract)\
                   .then_inc(negmax_ready, 1)

            def normalize(g):
                t, par = (g.r - 2) % T, g.r % 2
                quad_out = shared_ps[:, 0:QT * P].rearrange("p (q g k) -> p q g k", q=QT, g=G)
                vec.wait_ge(out_filled, g.s - 1)
                vec.reciprocal(rsum[:, par], quad_out[:, :, :, D:D + 1]).then_inc(rsum_ready, 1)
                vec.wait_ge(rsum_ready, g.s - 1)
                if g.project:
                    vec.wait_ge(attnT_filled, g.b + 1)
                vec.tensor_tensor(attn[:, :, G * D * t:G * D * (t + 1)].rearrange("p q (g k) -> p q g k", g=G),
                                  quad_out[:, :, :, 0:D], rsum[:, par].to_broadcast([P, QT, G, D]), ALU.mult)\
                   .then_inc(out_done, 1)

            def step(g):
                b, r, s = g.b, g.r, g.s
                if g.maxes:
                    reduce_unit(s + 1, EARLY, (r + 1) % 2)
                if g.project:
                    vec.wait_ge(proj_filled, b + 1)
                    vec.tensor_tensor(m.x[:, bass.ts(b, QT), :],
                                      shared_ps[:, 0:QT * C].rearrange("p (q c) -> p q c", c=C),
                                      m.x[:, bass.ts(b, QT), :], ALU.add).then_inc(proj_done, 1)
                if g.maxes:
                    for w in range(EARLY + 1, MAXES):
                        reduce_unit(s + 1, w, (r + 1) % 2)
                    negate_max(s + 1, (r + 1) % T, (r + 1) % 2)
                for w in range(EARLY):
                    if g.early_maxes:
                        reduce_unit(s + 2, w, r % 2)
                    if w == EARLY // 3 and g.output:
                        normalize(g)

            for w in range(MAXES):
                reduce_unit(0, w, 0)
            negate_max(0, 0, 0)
            for w in range(EARLY):
                reduce_unit(1, w, 1)
            steps(vec, step)

        @block.tensor
        def _(pe):
            def transpose_rows(s, t, half):
                if half == 0:
                    pe.wait_ge(rows_ready, s * 3 + 3)
                else:
                    pe.wait_ge(keys_copied, s * 2 + 1)
                for k in range(4 * half, 4 * half + 4):
                    tile = m.key_rows[:, t, k] if k < KT else m.query_rows[:, t, k - KT]
                    mm = pe.transpose(shared_r[:, (k % 4) * P:(k % 4 + 1) * P],
                                      tile.rearrange("p g k -> p (g k)"), m.ident_r[:])
                mm.then_inc(keys_filled, 1)

            def max_unit(s, w, t, wait=True):
                g, part = divmod(w, 3)
                if w == 0:
                    pe.wait_ge(keys_copied, s * 2 + 2)
                    pe.wait_ge(plain_copied, s * G + G)
                if wait:
                    pe.wait_ge(max_done, s * MAXES + (w - 1))
                if part < 2:
                    mm = pe.matmul(max_ps[w % 2][:], plain[t % 2][:, g, part * P:(part + 1) * P],
                                   m.keys[:, t, 0:NC_], start=True, stop=True)
                else:
                    for q in range(QT):
                        mm = pe.matmul(max_ps[w % 2][:, q * N:(q + 1) * N],
                                       plain[t % 2][:, g, q * P:(q + 1) * P], m.keys[:, t, NC_:KEYS],
                                       start=True, stop=True)
                mm.then_inc(max_filled, 1)

            def shift_rows(s, t):
                pe.wait_ge(negmax_ready, s + 1)
                for q in range(QT):
                    mm = pe.transpose(shared_r[:, q * P:(q + 1) * P],
                                      m.query_rows[:, t, q].rearrange("p g k -> p (g k)"), m.ident_r[:])
                mm.then_inc(shifted_filled, 1)

            def exp_unit(s, u, t, par, wait=True):
                if u == 0:
                    pe.wait_ge(shifted_copied, s * G + G)
                if wait:
                    pe.wait_ge(exp_done, s * UNITS + (u - 1))
                for half in range(UNIT_BANKS):
                    mm = pe.matmul(exp_ps[u % 2][:, half * BANK:(half + 1) * BANK], m.keys[:, t, u * P:(u + 1) * P],
                                   shifted[par][:, 2 * half:2 * half + 2, :], start=True, stop=True)
                mm.then_inc(exp_filled, 1)

            def pv_tile(s, k, t, par):
                if k == 0:
                    pe.wait_ge(exp_done, s * UNITS + UNITS)
                    pe.wait_ge(values_ready, s * 2 + 2)
                    pe.wait_ge(pv_copied, s)
                for g in range(G):
                    mm = pe.matmul(pv_ps[ROWS * g:ROWS * (g + 1), 0:N], m.value_cols[:, t, k, g, :],
                                   probs[par][:, k, g, :], start=(k == 0), stop=(k == KT - 1))
                if k == KT - 1:
                    mm.then_inc(pv_filled, 1)

            def step(g):
                b, r, s = g.b, g.r, g.s
                t, par = r % T, r % 2
                t1, t2 = (r + 1) % T, (r + 2) % T
                units = [(s + 1, w, t1) for w in range(EARLY, MAXES)] if g.maxes else []
                units += [(s + 2, w, t2) for w in range(EARLY)] if g.early_maxes else []

                def next_max():
                    if units:
                        max_unit(*units.pop(0))

                for u in range(UNITS):
                    next_max()
                    if u == 0 and g.project:
                        pe.wait_ge(attnT_copied, b + 1)
                        if g.early_maxes:
                            pe.wait_ge(plain_copied, s * G + 3 * G)
                        for q in range(QT):
                            mm = pe.matmul(shared_ps[:, q * C:(q + 1) * C], attnT[:, q, :], m.wproj[:],
                                           start=True, stop=True)
                        mm.then_inc(proj_filled, 1)
                    if u == SHIFT_SLOT and g.maxes:
                        if g.early_maxes:
                            pe.wait_ge(keys_copied, s * 2 + 6)
                            pe.wait_ge(plain_copied, s * G + 3 * G)
                        else:
                            pe.wait_ge(out_done, s - 2)
                        if g.project:
                            pe.wait_ge(proj_done, b + 1)
                        shift_rows(s + 1, t1)
                    if u == OUT_SLOT and g.output:
                        if g.maxes:
                            pe.wait_ge(shifted_copied, s * G + 2 * G)
                        else:
                            pe.wait_ge(out_done, s - 2)
                        pe.wait_ge(pv_copied, s - 1)
                        for q in range(QT):
                            mm = pe.transpose(shared_ps[:, q * P:(q + 1) * P], pv_sb[:, q * P:(q + 1) * P], m.ident[:])
                        mm.then_inc(out_filled, 1)
                    if u == ATTN_SLOT and g.transpose_out:
                        pe.wait_ge(out_done, s - 1)
                        for q in range(QT):
                            mm = pe.transpose(shared_ps[:, q * P:(q + 1) * P], attn[:, q, :], m.ident[:])
                        mm.then_inc(attnT_filled, 1)
                    if g.scores:
                        exp_unit(s, u, t, par, wait=r > 0 or u >= 2)
                    if u == KEYS_SLOT and g.transposes:
                        if g.output:
                            pe.wait_ge(out_done, s - 1)
                        else:
                            pe.wait_ge(shifted_copied, s * G + 2 * G)
                        if g.transpose_out:
                            pe.wait_ge(attnT_copied, b + 1)
                        transpose_rows(s + 3, (r + 3) % T, 0)
                    if u == QUERIES_SLOT and g.transposes:
                        transpose_rows(s + 3, (r + 3) % T, 1)
                    next_max()
                    if g.product:
                        for k in PV_SLOTS[u]:
                            pv_tile(s - 1, k, (r - 1) % T, 1 - par)

            transpose_rows(0, 0, 0)
            transpose_rows(0, 0, 1)
            for q in range(1, 2):
                pe.wait_ge(keys_copied, 2)
                pe.wait_ge(plain_copied, G)
                transpose_rows(q, q, 0)
                transpose_rows(q, q, 1)
            for w in range(MAXES):
                max_unit(0, w, 0, wait=w >= 2)
            pe.wait_ge(keys_copied, 4)
            pe.wait_ge(plain_copied, 2 * G)
            shift_rows(0, 0)
            pe.wait_ge(shifted_copied, G)
            transpose_rows(2, 2, 0)
            transpose_rows(2, 2, 1)
            for w in range(EARLY):
                max_unit(1, w, 1)
            steps(pe, step)


class Memory:

    def __init__(self, nc, ctx):
        sb = lambda name, shape, dt=F32: ctx.enter_context(nc.sbuf_tensor(name, shape, dt))
        self.x = sb("x", [P, TILES, C])
        self.gate, self.up = sb("gate", [P, E, I]), sb("up", [P, E, I])
        self.ones = sb("ones", [P, P])
        self.eps = sb("eps_sb", [P, 1])
        self.ident = sb("ident", [P, P])
        self.gate_up_in = ctx.enter_context(nc.semaphore("gate_up_in"))

    def for_attention(self, nc, ctx):
        sb = lambda name, shape, dt=F32: ctx.enter_context(nc.sbuf_tensor(name, shape, dt))
        self.context = sb("context", [P, B * CT, 2 * C])
        self.qkv = sb("qkv", [P, TILES, 3 * C])
        self.key_rows = sb("key_rows", [P, T, KT, G, ROWS], F32R)
        self.query_rows = sb("query_rows", [P, T, QT, G, ROWS], F32R)
        self.value_cols = sb("value_cols", [P, T, KT, G, ROWS])
        self.keys = sb("keys", [P, T, KEYS], F32R)
        self.wproj = sb("wproj", [P, C])
        self.bproj = sb("bproj", [1, C])
        self.bias = sb("bias", [P, C])
        self.ident_r = sb("ident_r", [P, P], F32R)
        self.context_in = [ctx.enter_context(nc.semaphore(f"context_in{b}")) for b in range(B)]


def build(nc, d, out):
    with ExitStack() as ctx:
        m = Memory(nc, ctx)
        with ExitStack() as attention:
            m.for_attention(nc, attention)
            project(nc, m, d)
            attend(nc, m, d)
        experts(nc, m, d, out)


SLOTS = (2 * TILES * P + E * (P - 1)) // P
SLOTS_PAD = -(-SLOTS // 4) * 4


def experts(nc, m, d, out):
    with ExitStack() as ctx:
        sem = lambda name: ctx.enter_context(nc.semaphore(name))
        sb = lambda name, shape, dt=F32: ctx.enter_context(nc.sbuf_tensor(name, shape, dt))
        psum = lambda name: ctx.enter_context(nc.psum_tensor(name, [P, BANK], F32))
        ln = [sem(n) for n in ("ln2_stats", "ln2_aggr", "ln2_std", "ln2_rstd", "ln2_norm")]
        router_in, down_in, const_start, const_ready = sem("router_in"), sem("down_in"), sem("const_start"), sem("const_ready")
        ht_filled, ht_copied = sem("ht_filled"), sem("ht_copied")
        const_filled, const_copied = sem("const_filled"), sem("const_copied")
        logits_filled, logits_done, conf_done = sem("logits_filled"), sem("logits_done"), sem("conf_done")
        gap_ready, weights_done = sem("gap_ready"), sem("weights_done")
        route = sem("route")
        picks_ready, place_filled, rows_placed, table_ready = sem("picks_ready"), sem("place_filled"), sem("rows_placed"), sem("table_ready")
        scattered, zeroed, mask_ready = sem("scattered"), sem("zeroed"), sem("mask_ready")
        gathered = [sem(f"gathered{i}") for i in range(TILES)]
        x_loaded = [sem(f"x_loaded{i}") for i in range(4)]
        y_stored = [sem(f"y_stored{i}") for i in range(4)]
        xT_filled, xT_copied = sem("xT_filled"), sem("xT_copied")
        gate_filled, up_filled = sem("gate_filled"), sem("up_filled")
        silu_done, act_done = sem("silu_done"), sem("act_done")
        actT_filled, actT_copied = sem("actT_filled"), sem("actT_copied")
        y_filled, y_copied = sem("y_filled"), sem("y_copied")
        summed, stored = sem("summed"), sem("stored")

        rows_dram = nc.dram_tensor("expert_rows", (SLOTS_PAD * P, C), F32, kind="Internal").ap()
        outs_dram = nc.dram_tensor("expert_outs", (SLOTS_PAD * P, C), F32, kind="Internal").ap()
        stats, aggr, rstd = sb("ln2_stats_sb", [P, TILES, 6]), sb("ln2_aggr_sb", [P, TILES, 2]), sb("ln2_rstd_sb", [P, 2, TILES])
        h = sb("h", [P, TILES, C])
        hT = sb("hT", [P, TILES * P])
        down = sb("down", [P, E, IC, C])
        conf_w = sb("conf_w", [P, E])
        conf_rows = sb("conf_rows", [1, 2 * E])
        conf_all = sb("conf_all", [P, 2, E])
        earlier = sb("earlier", [P, E, E])
        before = sb("before", [P, P])
        zeros = sb("zeros", [P, SLOTS_PAD * C // 4])
        tile_start = sb("tile_start", [P, E, TILES])
        slot_index = sb("slot_index", [1, SLOTS_PAD, E])
        z, bids = sb("z", [P, TILES, E]), sb("bids", [P, TILES, E])
        pair, pair2 = sb("pair", [P, TILES, E, E]), sb("pair2", [P, TILES, E, E])
        rank = sb("rank", [P, TILES, E])
        top = sb("top", [P, 2, TILES, E])
        picked = sb("picked", [P, 2, TILES, E])
        best = sb("best", [P, 2, TILES, 1])
        gap, weight = sb("gap", [P, 2, TILES, 1]), sb("weight", [P, 2, TILES, 1])
        picks = sb("picks", [P, TILES + 1, E])
        place = sb("place", [P, TILES, E])
        row_f, row = sb("row_f", [P, 2, TILES]), sb("row", [P, 2, TILES], mybir.dt.uint32)
        count, full = sb("count", [P, E]), sb("full", [P, E, TILES])
        tiles_of, first, end = sb("tiles_of", [P, E]), sb("first_slot", [P, E]), sb("end_slot", [P, E])
        before_e = sb("before_e", [P, E, E])
        ended, slot_e = sb("ended", [1, SLOTS_PAD, E]), sb("slot_e", [1, SLOTS_PAD])
        table = sb("table", [1, SLOTS_PAD], I32)
        x_in = sb("x_in", [P, 4, C])
        xT = sb("xT", [P, 2, P])
        silu, hidden = sb("silu", [P, 2, I]), sb("hidden", [P, 2, I])
        hiddenT = sb("hiddenT", [P, 2, IC, P])
        y_out = sb("y_out", [P, 4, C])
        y_in = sb("y_in", [P, 2, TILES, C])
        t_ps = [psum(f"t_ps{i}") for i in range(2)]
        gate_ps, up_ps = [psum(f"gate_ps{i}") for i in range(2)], [psum(f"up_ps{i}") for i in range(2)]
        at_ps = [psum(f"at_ps{i}") for i in range(2)]
        xT_ps, y_ps = t_ps
        CONSTS = 4
        block = ctx.enter_context(nc.Block())

        def slots(engine, step, last):
            for j in range(4):
                step(0, j)
            with engine.Fori(1, SLOTS_PAD // 4 - 1) as i:
                for r in range(4):
                    step(i, r)
            for r in range(last - (SLOTS_PAD - 4)):
                step(SLOTS_PAD // 4 - 1, r)

        def exists(i, r, shift):
            return not isinstance(i, int) or 0 <= 4 * i + r + shift < SLOTS_PAD

        @block.sync
        def _(sp):
            sp.dma_start(conf_w[:], d["conf_wT"]).then_inc(router_in, 16)
            sp.dma_start(conf_rows[:, 0:E], d["conf_b"].rearrange("(a e) -> a e", a=1)).then_inc(router_in, 16)
            sp.dma_start(conf_rows[:, E:2 * E], d["wealth"].rearrange("(a e) -> a e", a=1)).then_inc(router_in, 16)
            sp.dma_start(down[:], d["downT"].rearrange("e (c p) h -> p e c h", p=P)).then_inc(down_in, 16)
            sp.wait_ge(const_ready, CONSTS)
            for k in range(4):
                sp.dma_start(rows_dram[k * SLOTS_PAD // 4 * P:(k + 1) * SLOTS_PAD // 4 * P, :]
                             .rearrange("(p n) c -> p (n c)", p=P), zeros[:]).then_inc(zeroed, 16)
            sp.wait_ge(scattered, 16 * 2 * TILES)

            def load(i, r, shift):
                j, r4 = 4 * i + r + shift, (r + shift) % 4
                wait_for(sp, xT_filled, j - 3)
                sp.dma_start(x_in[:, r4, :], rows_dram[bass.ts(j, P), :]).then_inc(x_loaded[r4], 16)

            def step(i, r):
                j = 4 * i + r
                if exists(i, r, 3):
                    load(i, r, 3)
                if exists(i, r, -2):
                    sp.wait_ge(y_copied, j - 1)
                    sp.dma_start(outs_dram[bass.ts(j - 2, P), :], y_out[:, (r - 2) % 4, :])\
                      .then_inc(y_stored[(r - 2) % 4], 16)

            for j in range(3):
                load(0, 0, j)
            slots(sp, step, SLOTS_PAD + 2)

        @block.gpsimd
        def _(pool):
            pool.memset(earlier[:], 1.0).then_inc(const_start, 1)
            pool.memset(before[:], 1.0).then_inc(const_start, 1)
            pool.memset(zeros[:], 0.0).then_inc(const_ready, 1)
            pool.iota(tile_start[:], pattern=[[0, E], [P, TILES]], base=0, channel_multiplier=0,
                      allow_small_or_imprecise_dtypes=True).then_inc(const_ready, 1)
            pool.iota(slot_index[:], pattern=[[1, SLOTS_PAD], [0, E]], base=0, channel_multiplier=0,
                      allow_small_or_imprecise_dtypes=True).then_inc(const_ready, 1)
            pool.memset(picks[:, TILES, :], 0.0).then_inc(const_ready, 1)
            pool.wait_ge(const_start, 2)
            pool.affine_select(out=earlier[:], in_=earlier[:], compare_op=ALU.is_gt, fill=0.0, base=0,
                               pattern=[[1, E], [-1, E]], channel_multiplier=0).then_inc(mask_ready, 1)
            pool.affine_select(out=before[:], in_=before[:], compare_op=ALU.is_gt, fill=0.0, base=0,
                               pattern=[[1, P]], channel_multiplier=-1).then_inc(mask_ready, 1)
            pool.wait_ge(ln[4], TILES)
            pool.wait_ge(rows_placed, 1)
            pool.wait_ge(zeroed, 64)
            for t in range(TILES):
                for k in range(2):
                    pool.indirect_dma_start(rows_dram, bass.IndirectOffsetOnAxis(ap=row[:, k, t:t + 1], axis=0),
                                            h[:, t, :], None).then_inc(scattered, 16)
            for r in range(4):
                pool.wait_ge(y_stored[r], 16 * (SLOTS_PAD // 4))
            for t in range(TILES):
                for k in range(2):
                    pool.indirect_dma_start(y_in[:, k, t, :], None, outs_dram,
                                            bass.IndirectOffsetOnAxis(ap=row[:, k, t:t + 1], axis=0))\
                        .then_inc(gathered[t], 16)

        @block.scalar
        def _(act):
            _, scalar_std, _ = layernorm(None, act, m.x, h, stats, aggr, rstd, ln)
            scalar_std(m.eps[:])
            for k in range(4):
                act.wait_ge(ht_filled, k + 1)
                act.activation(hT[:, k * BANK:(k + 1) * BANK], t_ps[k % 2][:], ACT.Copy).then_inc(ht_copied, 1)
            act.wait_ge(logits_done, 1)
            act.activation(bids[:], z[:], ACT.Sigmoid).then_inc(conf_done, 1)
            act.wait_ge(gap_ready, 2)
            act.activation(weight[:], gap[:], ACT.Sigmoid).then_inc(weights_done, 1)

            def step(i, r):
                j = 4 * i + r
                if exists(i, r, 0):
                    act.wait_ge(gate_filled, j + 1)
                    wait_for(act, act_done, j - 1)
                    act.activation(silu[:, r % 2, :], gate_ps[r % 2][:], ACT.Silu).then_inc(silu_done, 1)
                if exists(i, r, -1):
                    act.wait_ge(actT_filled, j)
                    wait_for(act, y_filled, j - 2)
                    act.activation(hiddenT[:, (r - 1) % 2], at_ps[(r - 1) % 2][:].rearrange("p (c n) -> p c n", n=P),
                                   ACT.Copy).then_inc(actT_copied, 1)

            slots(act, step, SLOTS_PAD + 1)
            act.wait_ge(summed, 2 * TILES)
            act.dma_start(out.rearrange("b (t p) c -> p (b t) c", p=P), m.x[:]).then_inc(stored, 16)
            act.wait_ge(stored, 16)

        @block.vector
        def _(vec):
            vector_stats, _, vector_norm = layernorm(vec, None, m.x, h, stats, aggr, rstd, ln)
            vector_stats()
            for i in range(TILES):
                vector_norm(i, first=i == 0)
            vec.wait_ge(const_filled, 1)
            vec.tensor_copy(conf_all[:], t_ps[0][:, 0:2 * E].rearrange("p (k e) -> p k e", e=E)).then_inc(const_copied, 1)
            vec.wait_ge(const_copied, 1)
            vec.wait_ge(logits_filled, 1)
            over_tiles = lambda ap: ap.unsqueeze(1).to_broadcast([P, TILES, E])
            vec.tensor_tensor(z[:], t_ps[1][:, 0:TILES * E].rearrange("p (t e) -> p t e", e=E),
                              over_tiles(conf_all[:, 0, :]), ALU.add).then_inc(logits_done, 1)
            steps = [0]

            def then(op):
                steps[0] += 1
                op.then_inc(route, 1)
                vec.wait_ge(route, steps[0])

            vec.wait_ge(conf_done, 1)
            then(vec.tensor_tensor(bids[:], bids[:], over_tiles(conf_all[:, 1, :]), ALU.mult))
            pairs = [P, TILES, E, E]
            this, other = bids[:].unsqueeze(3).to_broadcast(pairs), bids[:].unsqueeze(2).to_broadcast(pairs)
            vec.wait_ge(mask_ready, 2)
            vec.wait_ge(const_ready, CONSTS)
            vec.tensor_tensor(pair2[:], other, this, ALU.is_gt)
            then(vec.tensor_tensor(pair[:], other, this, ALU.is_equal))
            then(vec.tensor_tensor(pair[:], pair[:], earlier[:].unsqueeze(1).to_broadcast(pairs), ALU.mult))
            then(vec.tensor_tensor(pair[:], pair[:], pair2[:], ALU.add))
            then(vec.tensor_reduce(rank[:], pair[:], axis=AX.X, op=ALU.add))
            vec.tensor_scalar(picks[:, 0:TILES, :], rank[:], 1.5, None, ALU.is_lt).then_inc(picks_ready, 1)
            for k in range(2):
                op = vec.tensor_scalar(top[:, k], rank[:], float(k), None, ALU.is_equal)
            then(op)
            for k in range(2):
                op = vec.tensor_tensor(picked[:, k], top[:, k], bids[:], ALU.mult)
            then(op)
            then(vec.tensor_reduce(best[:, :, :, 0], picked[:], axis=AX.X, op=ALU.add))
            for k in range(2):
                vec.tensor_tensor(gap[:, k], best[:, k], best[:, 1 - k], ALU.subtract).then_inc(gap_ready, 1)
            vec.wait_ge(place_filled, 1)
            then(vec.tensor_copy(count[:], t_ps[0][:, TILES * E:(TILES + 1) * E]))
            then(vec.tensor_tensor(full[:], count[:].unsqueeze(2).to_broadcast([P, E, TILES]), tile_start[:], ALU.is_gt))
            then(vec.tensor_reduce(tiles_of[:], full[:], axis=AX.X, op=ALU.add))
            then(vec.tensor_tensor(before_e[:], earlier[:], tiles_of[:].unsqueeze(1).to_broadcast([P, E, E]), ALU.mult))
            then(vec.tensor_reduce(first[:], before_e[:], axis=AX.X, op=ALU.add))
            then(vec.scalar_tensor_tensor(place[:], over_tiles(first[:]), float(P),
                                          t_ps[0][:, 0:TILES * E].rearrange("p (t e) -> p t e", e=E),
                                          ALU.mult, ALU.add))
            for k in range(2):
                op = vec.tensor_tensor(picked[:, k], top[:, k], place[:], ALU.mult)
            then(op)
            then(vec.tensor_reduce(row_f[:], picked[:], axis=AX.X, op=ALU.add))
            vec.tensor_copy(row[:], row_f[:]).then_inc(rows_placed, 1)
            then(vec.tensor_tensor(end[:], first[:], tiles_of[:], ALU.add))
            then(vec.tensor_tensor(ended[:], slot_index[:], end[0:1].unsqueeze(1).to_broadcast([1, SLOTS_PAD, E]), ALU.is_ge))
            then(vec.tensor_reduce(slot_e[:], ended[:, :, 0:E - 1], axis=AX.X, op=ALU.add))
            vec.tensor_copy(table[:], slot_e[:]).then_inc(table_ready, 1)

            def copy_xT(j, r):
                vec.wait_ge(xT_filled, j + 1)
                wait_for(vec, up_filled, j - 1)
                vec.tensor_copy(xT[:, r % 2, :], xT_ps[:, 0:P]).then_inc(xT_copied, 1)

            def step(i, r):
                j = 4 * i + r
                if exists(i, r, 0):
                    vec.wait_ge(silu_done, j + 1)
                    vec.wait_ge(up_filled, j + 1)
                    wait_for(vec, actT_filled, j - 1)
                    vec.tensor_tensor(hidden[:, r % 2, :], up_ps[r % 2][:], silu[:, r % 2, :], ALU.mult)\
                       .then_inc(act_done, 1)
                if exists(i, r, 1):
                    copy_xT(j + 1, r + 1)
                if exists(i, r, -2):
                    vec.wait_ge(y_filled, j - 1)
                    if not isinstance(i, int) or j >= 6:
                        vec.wait_ge(y_stored[(r - 2) % 4], (i if r >= 2 else i - 1) * 16)
                    vec.tensor_copy(y_out[:, (r - 2) % 4, :], y_ps[:, 0:C]).then_inc(y_copied, 1)

            copy_xT(0, 0)
            slots(vec, step, SLOTS_PAD + 2)
            for t in range(TILES):
                vec.wait_ge(gathered[t], 32)
                if t == 0:
                    vec.wait_ge(weights_done, 1)
                for k in range(2):
                    if k:
                        vec.wait_ge(summed, 2 * t + 1)
                    vec.scalar_tensor_tensor(m.x[:, t, :], y_in[:, k, t, :], weight[:, k, t, :], m.x[:, t, :],
                                             ALU.mult, ALU.add).then_inc(summed, 1)

        @block.tensor
        def _(pe):
            for k in range(4):
                pe.wait_ge(ln[4], (k + 1) * 4)
                if k >= 2:
                    pe.wait_ge(ht_copied, k - 1)
                for i in range(4):
                    mm = pe.transpose(t_ps[k % 2][:, i * P:(i + 1) * P], h[:, k * 4 + i, :], m.ident[:])
                mm.then_inc(ht_filled, 1)
            pe.wait_ge(ht_copied, 4)
            pe.wait_ge(router_in, 48)
            pe.matmul(t_ps[0][:, 0:2 * E], m.ones[0:1, :], conf_rows[0:1, :], start=True, stop=True)\
              .then_inc(const_filled, 1)
            for i in range(TILES):
                mm = pe.matmul(t_ps[1][:, i * E:(i + 1) * E], hT[:, i * P:(i + 1) * P], conf_w[:], start=True, stop=True)
            mm.then_inc(logits_filled, 1)
            pe.wait_ge(picks_ready, 1)
            pe.wait_ge(const_copied, 1)
            pe.matmul(t_ps[0][:, 0:(TILES + 1) * E], before[:], picks[:].rearrange("p t e -> p (t e)"),
                      start=True, stop=False)
            for t in range(TILES):
                n = TILES - t
                mm = pe.matmul(t_ps[0][:, (t + 1) * E:(TILES + 1) * E], m.ones[:],
                               picks[:, t, :].unsqueeze(1).to_broadcast([P, n, E]), start=False, stop=(t == TILES - 1))
            mm.then_inc(place_filled, 1)
            pe.wait_ge(rows_placed, 1)
            pe.wait_ge(logits_done, 1)
            pe.wait_ge(m.gate_up_in, 32)
            pe.wait_ge(down_in, 16)
            pe.wait_ge(table_ready, 1)

            def expert(j):
                return pe.value_load(table[0:1, bass.ds(j, 1)], min_val=0, max_val=E - 1)

            def transpose_x(i, r, shift):
                j, r4 = 4 * i + r + shift, (r + shift) % 4
                pe.wait_ge(x_loaded[r4], (i + (r + shift) // 4) * 16 + 16)
                wait_for(pe, xT_copied, j)
                pe.transpose(xT_ps[:, 0:P], x_in[:, r4, :], m.ident[:]).then_inc(xT_filled, 1)

            def step(i, r):
                j = 4 * i + r
                if exists(i, r, 0):
                    e = expert(j)
                    pe.wait_ge(xT_copied, j + 1)
                    wait_for(pe, silu_done, j - 1)
                    pe.matmul(gate_ps[r % 2][:], xT[:, r % 2, :], m.gate[:, bass.ds(e, 1), :].rearrange("p a i -> p (a i)"),
                              start=True, stop=True).then_inc(gate_filled, 1)
                    wait_for(pe, act_done, j - 1)
                    pe.matmul(up_ps[r % 2][:], xT[:, r % 2, :], m.up[:, bass.ds(e, 1), :].rearrange("p a i -> p (a i)"),
                              start=True, stop=True).then_inc(up_filled, 1)
                if exists(i, r, 1):
                    transpose_x(i, r, 1)
                if exists(i, r, -2):
                    e = expert(j - 2)
                    pe.wait_ge(actT_copied, j - 1)
                    wait_for(pe, y_copied, j - 2)
                    for c in range(IC):
                        mm = pe.matmul(y_ps[:, 0:C], hiddenT[:, r % 2, c, :],
                                       down[:, bass.ds(e, 1), c, :].rearrange("p a h -> p (a h)"),
                                       start=(c == 0), stop=(c == IC - 1))
                    mm.then_inc(y_filled, 1)
                if exists(i, r, -1):
                    pe.wait_ge(act_done, j)
                    wait_for(pe, actT_copied, j - 2)
                    for c in range(IC):
                        mm = pe.transpose(at_ps[(r - 1) % 2][:, c * P:(c + 1) * P],
                                          hidden[:, (r - 1) % 2, c * P:(c + 1) * P], m.ident[:])
                    mm.then_inc(actT_filled, 1)

            transpose_x(0, 0, 0)
            slots(pe, step, SLOTS_PAD + 2)


def kernel(x, ctx_2048, L0_xattn_w_qkv, L0_xattn_w_proj, L0_xattn_b_proj, L0_ffn_conf_w, L0_ffn_conf_b,
           L0_ffn_gate_w, L0_ffn_up_w, L0_ffn_down_w, L0_ffn_wealth):
    import concourse.bacc as bacc
    from concourse.bass_utils import run_bass_kernel_spmd

    t = lambda a: np.ascontiguousarray(np.swapaxes(np.asarray(a), -1, -2))
    arrays = {
        "x": np.asarray(x), "ctx": np.asarray(ctx_2048), "w_qkvT": t(L0_xattn_w_qkv),
        "w_projT": t(L0_xattn_w_proj), "b_proj": np.asarray(L0_xattn_b_proj),
        "conf_wT": t(L0_ffn_conf_w), "conf_b": np.asarray(L0_ffn_conf_b), "wealth": np.asarray(L0_ffn_wealth),
        "gateT": t(L0_ffn_gate_w), "upT": t(L0_ffn_up_w), "downT": t(L0_ffn_down_w),
    }
    nc = bacc.Bacc("TRN2", target_bir_lowering=False, num_devices=1)
    d = {k: nc.dram_tensor(f"{k}_dram", a.shape, mybir.dt.from_np(a.dtype), kind="ExternalInput").ap() for k, a in arrays.items()}
    out = nc.dram_tensor("out_dram", (B, N, C), F32, kind="ExternalOutput").ap()
    build(nc, d, out)
    r = run_bass_kernel_spmd(nc, [{f"{k}_dram": a for k, a in arrays.items()}], core_ids=[0])
    return r.results[0]["out_dram"]
```

```python
from contextlib import ExitStack

import numpy as np

import concourse.bass as bass
from concourse import mybir

F32 = mybir.dt.float32
F32R = mybir.dt.float32r
I32 = mybir.dt.int32
ALU = mybir.AluOpType
ACT = mybir.ActivationFunctionType
AX = mybir.AxisListType

P = 128
B, N, C = 8, 256, 128
NC_ = 512
HEADS, D = 16, 8
QT = N // P
CT = NC_ // P
KT = CT + QT
KEYS = KT * P
TILES = B * QT
G = 4
T = HEADS // G
QUADS = B * T
ROWS = 32
SPLIT = 3 * D
SCALE = float(D) ** -0.5
EPS = 1e-5
E, I = 8, 512
IC = I // P
BANK = 512


def wait_for(engine, sem, value):
    if not isinstance(value, int) or value > 0:
        engine.wait_ge(sem, value)


def layernorm(vec, act, src, dst, stats, aggr, rstd, done):
    stats_in, aggr_in, std_in, rstd_in, norm_out = done

    def vector_stats():
        for i in range(TILES):
            vec.bn_stats(stats[:, i, :], src[:, i, :])\
               .then_inc(stats_in, 1)
        for i in range(TILES):
            vec.wait_ge(stats_in, i + 1)
            vec.bn_aggr(aggr[:, i, :], stats[:, i, :]).then_inc(aggr_in, 1)

    def scalar_std(eps):
        act.wait_ge(aggr_in, TILES)
        act.activation(rstd[:, 0, :], aggr[:, :, 1], ACT.Sqrt, bias=eps, scale=1.0).then_inc(std_in, 1)

    def vector_norm(i, first=False):
        if first:
            vec.wait_ge(std_in, 1)
            vec.reciprocal(rstd[:, 1, :], rstd[:, 0, :]).then_inc(rstd_in, 1)
            vec.wait_ge(rstd_in, 1)
        vec.tensor_scalar(dst[:, i, :], src[:, i, :], aggr[:, i, 0:1], rstd[:, 1, i:i + 1],
                          ALU.subtract, ALU.mult).then_inc(norm_out, 1)

    return vector_stats, scalar_std, vector_norm


def project(nc, m, d):
    with ExitStack() as ctx:
        sem = lambda name: ctx.enter_context(nc.semaphore(name))
        x_in, w_in = sem("x_in"), sem("w_in")
        ident_zero, ident_done, const_done = sem("ident_zero"), sem("ident_done"), sem("const_done")
        ln = [sem(n) for n in ("ln1_stats", "ln1_aggr", "ln1_std", "ln1_rstd", "ln1_norm")]
        xt_filled, xt_copied = sem("xt_filled"), sem("xt_copied")
        qkv_filled, qkv_copied = sem("qkv_filled"), sem("qkv_copied")
        bias_filled, bias_copied = sem("bias_filled"), sem("bias_copied")
        stats = ctx.enter_context(nc.sbuf_tensor("ln1_stats_sb", [P, TILES, 6], F32))
        aggr = ctx.enter_context(nc.sbuf_tensor("ln1_aggr_sb", [P, TILES, 2], F32))
        rstd = ctx.enter_context(nc.sbuf_tensor("ln1_rstd_sb", [P, 2, TILES], F32))
        xn = ctx.enter_context(nc.sbuf_tensor("xn", [P, TILES, C], F32))
        xnT = ctx.enter_context(nc.sbuf_tensor("xnT", [P, 2, P], F32))
        wqkv = ctx.enter_context(nc.sbuf_tensor("wqkv", [P, 3 * C], F32))
        xt_ps = [ctx.enter_context(nc.psum_tensor(f"xt_ps{i}", [P, BANK], F32)) for i in range(2)]
        qkv_ps = [ctx.enter_context(nc.psum_tensor(f"qkv_ps{i}", [P, BANK], F32)) for i in range(2)]
        block = ctx.enter_context(nc.Block())

        @block.sync
        def _(sp):
            sp.dma_start(m.x[:], d["x"].rearrange("b (t p) c -> p (b t) c", p=P)).then_inc(x_in, 16)
            sp.dma_start(wqkv[:], d["w_qkvT"]).then_inc(w_in, 16)
            sp.dma_start(m.wproj[:], d["w_projT"]).then_inc(w_in, 16)
            sp.dma_start(m.bproj[:], d["b_proj"].rearrange("(a c) -> a c", a=1)).then_inc(w_in, 16)
            for b in range(B):
                sp.dma_start(m.context[:, b * CT:(b + 1) * CT, :],
                             d["ctx"][b].rearrange("(t p) f -> p t f", p=P)).then_inc(m.context_in[b], 16)
            for w, src in ((m.gate, "gateT"), (m.up, "upT")):
                sp.dma_start(w[:], d[src].rearrange("e p i -> p e i")).then_inc(m.gate_up_in, 16)

        @block.gpsimd
        def _(pool):
            pool.memset(m.ident[:], 0.0).then_inc(ident_zero, 1)
            pool.memset(m.ones[:], 1.0).then_inc(const_done, 1)
            pool.memset(m.eps[:], EPS).then_inc(const_done, 1)
            pool.wait_ge(ident_zero, 1)
            pool.affine_select(out=m.ident[:], in_=m.ident[:], compare_op=ALU.not_equal, fill=1.0, base=0,
                               pattern=[[-1, P]], channel_multiplier=1).then_inc(ident_done, 1)
            pool.wait_ge(ident_done, 1)
            pool.tensor_copy(m.ident_r[:], m.ident[:]).then_inc(ident_done, 1)
            pool.memset(m.key_rows[:, :, :, :, SPLIT:SPLIT + 2].bitcast(F32), 1.0).then_inc(const_done, 1)
            pool.memset(m.key_rows[:, :, :, :, SPLIT + 2:ROWS].bitcast(F32), 0.0).then_inc(const_done, 1)
            pool.memset(m.query_rows[:, :, :, :, SPLIT:ROWS].bitcast(F32), 0.0).then_inc(const_done, 1)
            pool.memset(m.value_cols[:, :, :, :, D:D + 1], 1.0).then_inc(const_done, 1)
            pool.memset(m.value_cols[:, :, :, :, D + 1:ROWS], 0.0).then_inc(const_done, 1)

        @block.vector
        def _(vec):
            vector_stats, _, vector_norm = layernorm(vec, None, m.x, xn, stats, aggr, rstd, ln)
            vec.wait_ge(x_in, 16)
            vector_stats()
            vector_norm(0, first=True)
            vector_norm(1)
            vec.wait_ge(bias_filled, 1)
            vec.tensor_copy(m.bias[:], xt_ps[0][:, 0:C]).then_inc(bias_copied, 1)
            for i in range(TILES):
                if i + 2 < TILES:
                    vector_norm(i + 2)
                vec.wait_ge(xt_filled, i + 1)
                if i >= 2:
                    vec.wait_ge(qkv_filled, i - 1)
                vec.tensor_copy(xnT[:, i % 2, :], xt_ps[i % 2][:, 0:P]).then_inc(xt_copied, 1)
            vec.wait_ge(bias_copied, 1)
            vec.tensor_tensor(m.x[:], m.x[:], m.bias[:].unsqueeze(1).to_broadcast([P, TILES, C]), ALU.add)

        @block.scalar
        def _(act):
            _, scalar_std, _ = layernorm(None, act, m.x, xn, stats, aggr, rstd, ln)
            act.wait_ge(const_done, 2)
            scalar_std(m.eps[:])
            for i in range(TILES):
                act.wait_ge(qkv_filled, i + 1)
                act.activation(m.qkv[:, i, 0:C], qkv_ps[i % 2][:, 0:C], ACT.Copy, scale=SCALE)
                act.activation(m.qkv[:, i, C:3 * C], qkv_ps[i % 2][:, C:3 * C], ACT.Copy).then_inc(qkv_copied, 1)

        @block.tensor
        def _(pe):
            pe.wait_ge(w_in, 48)
            pe.wait_ge(const_done, 1)
            pe.matmul(xt_ps[0][:, 0:C], m.ones[0:1, :], m.bproj[0:1, :], start=True, stop=True).then_inc(bias_filled, 1)
            pe.wait_ge(ident_done, 1)
            for i in range(TILES + 1):
                if i < TILES:
                    pe.wait_ge(ln[4], i + 1)
                    if i == 0:
                        pe.wait_ge(bias_copied, 1)
                    if i >= 2:
                        pe.wait_ge(xt_copied, i - 1)
                    pe.transpose(xt_ps[i % 2][:, 0:P], xn[:, i, :], m.ident[:]).then_inc(xt_filled, 1)
                if i >= 1:
                    j = i - 1
                    pe.wait_ge(xt_copied, j + 1)
                    if j >= 2:
                        pe.wait_ge(qkv_copied, j - 1)
                    pe.matmul(qkv_ps[j % 2][:, 0:3 * C], xnT[:, j % 2, :], wqkv[:], start=True, stop=True)\
                      .then_inc(qkv_filled, 1)


UNIT_BANKS = 2
UNITS = KT
MAXES = 3 * G
EARLY = 3 * MAXES // 4
SHIFT_SLOT, OUT_SLOT, ATTN_SLOT, KEYS_SLOT, QUERIES_SLOT = 2, 3, 4, 4, 5
PV_BEFORE = [(4,), (5,), (), (), (), ()]
PV_NOW = [(), (), (0,), (1,), (2,), (3,)]


def attend(nc, m, d):
    with ExitStack() as ctx:
        sem = lambda name: ctx.enter_context(nc.semaphore(name))
        high_ready = sem("high_ready")
        rows_ready = sem("rows_ready")
        values_ready = sem("values_ready")
        keys_filled, keys_copied = sem("keys_filled"), sem("keys_copied")
        plain_copied = sem("plain_copied")
        max_filled, max_done = sem("max_filled"), sem("max_done")
        negmax_ready = sem("negmax_ready")
        shifted_filled, shifted_copied = sem("shifted_filled"), sem("shifted_copied")
        exp_filled, exp_done = sem("exp_filled"), sem("exp_done")
        pv_filled, pv_copied = sem("pv_filled"), sem("pv_copied")
        out_filled, out_done = sem("out_filled"), sem("out_done")
        attnT_filled, attnT_copied = sem("attnT_filled"), sem("attnT_copied")
        proj_filled, proj_done = sem("proj_filled"), sem("proj_done")
        blocks_zero = sem("blocks_zero")
        chain = sem("chain")
        rsum_ready = sem("rsum_ready")
        max_part = ctx.enter_context(nc.sbuf_tensor("max_part", [P, 2, G, 2, QT], F32))
        rowmax = ctx.enter_context(nc.sbuf_tensor("rowmax", [P, 2, G, QT], F32))
        plain = [ctx.enter_context(nc.sbuf_tensor(f"plain{i}", [P, G, N], F32R)) for i in range(2)]
        shifted = [ctx.enter_context(nc.sbuf_tensor(f"shifted{i}", [P, G, N], F32R)) for i in range(2)]
        probs = [ctx.enter_context(nc.sbuf_tensor(f"probs{i}", [P, KT, G, N], F32)) for i in range(2)]
        pv_sb = ctx.enter_context(nc.sbuf_tensor("pv_sb", [P, N], F32))
        rsum = ctx.enter_context(nc.sbuf_tensor("rsum", [P, 2, QT, G, 1], F32))
        attn = ctx.enter_context(nc.sbuf_tensor("attn", [P, QT, C], F32))
        attnT = ctx.enter_context(nc.sbuf_tensor("attnT", [P, QT, P], F32))
        exp_ps = [ctx.enter_context(nc.psum_tensor(f"exp_ps{i}", [P, UNIT_BANKS * BANK], F32)) for i in range(2)]
        max_ps = [ctx.enter_context(nc.psum_tensor(f"max_ps{i}", [P, BANK], F32)) for i in range(2)]
        pv_ps = ctx.enter_context(nc.psum_tensor("pv_ps", [P, BANK], F32))
        shared_ps = ctx.enter_context(nc.psum_tensor("shared_ps", [P, BANK], F32))
        shared_r = shared_ps[:].bitcast(F32R)
        block = ctx.enter_context(nc.Block())

        def steps(engine, step):
            for s in range(3):
                step(Step(0, s))
            with engine.Fori(0, B - 2) as b:
                for r in range(3, T + 3):
                    step(Step(b, r))
            for b in range(B - 2, B):
                for r in range(3, T + 3):
                    step(Step(b, r))

        class Step:

            def __init__(self, b, r):
                self.b, self.r, self.s = b, r, b * T + r
                inner = not isinstance(b, int)
                self.transposes = inner or self.s + 3 < QUADS
                self.early_maxes = inner or self.s + 2 < QUADS
                self.maxes = inner or self.s + 1 < QUADS
                self.scores = inner or self.s < QUADS
                self.output = inner or 1 <= self.s <= QUADS
                self.transpose_out = r == T
                self.project = r == T + 1

        @block.gpsimd
        def _(pool):
            heads = lambda ap: ap.rearrange("p k (g d) -> p k g d", d=D)

            def fill_rows(b, t, values):
                cols = lambda first: slice(first + G * D * t, first + G * D * (t + 1))
                ctx_k = heads(m.context[:, bass.ts(b, CT), cols(0)])
                own_k = heads(m.qkv[:, bass.ts(b, QT), cols(C)])
                own_q = heads(m.qkv[:, bass.ts(b, QT), cols(0)])
                kr, qr = m.key_rows[:, t], m.query_rows[:, t]
                for src, dst in ((ctx_k, kr[:, 0:CT]), (own_k, kr[:, CT:KT])):
                    pool.tensor_copy(dst[:, :, :, 0:D], src).then_inc(high_ready, 1)
                    pool.tensor_copy(dst[:, :, :, 2 * D:3 * D], src).then_inc(high_ready, 1)
                pool.tensor_copy(qr[:, :, :, 0:D], own_q).then_inc(high_ready, 1)
                pool.tensor_copy(qr[:, :, :, D:2 * D], own_q).then_inc(high_ready, 1)
                values()
                pool.tensor_tensor(kr[:, 0:CT, :, D:2 * D], ctx_k, kr[:, 0:CT, :, 0:D], ALU.subtract)\
                    .then_inc(rows_ready, 1)
                pool.tensor_tensor(kr[:, CT:KT, :, D:2 * D], own_k, kr[:, CT:KT, :, 0:D], ALU.subtract)\
                    .then_inc(rows_ready, 1)
                pool.tensor_tensor(qr[:, :, :, 2 * D:3 * D], own_q, qr[:, :, :, 0:D], ALU.subtract)\
                    .then_inc(rows_ready, 1)

            def fill_values(b, t):
                cols = lambda first: slice(first + G * D * t, first + G * D * (t + 1))
                pool.tensor_copy(m.value_cols[:, t, 0:CT, :, 0:D], heads(m.context[:, bass.ts(b, CT), cols(C)]))\
                    .then_inc(values_ready, 1)
                pool.tensor_copy(m.value_cols[:, t, CT:KT, :, 0:D], heads(m.qkv[:, bass.ts(b, QT), cols(2 * C)]))\
                    .then_inc(values_ready, 1)

            for half in plain + shifted:
                pool.memset(half[:].bitcast(F32), 0.0).then_inc(blocks_zero, 1)
            for b in range(B):
                pool.wait_ge(m.context_in[b], 16)
            def fill_quad(b, t):
                s = b * T + t

                def values():
                    if not (isinstance(b, int) and b == 0 and t == 0):
                        wait_for(pool, pv_filled, s - T)
                        pool.wait_ge(high_ready, s * 6 + 6)
                        fill_values(b if t else b - 1, (t - 1) % T)
                    else:
                        pool.wait_ge(high_ready, 6)
                fill_rows(b, t, values)

            for t in range(T):
                fill_quad(0, t)
            for t in range(T):
                pool.wait_ge(shifted_filled, t + 1)
                fill_quad(1, t)
            with pool.Fori(2, B) as b:
                for t in range(T):
                    pool.wait_ge(shifted_filled, b * T + (t - T + 1))
                    fill_quad(b, t)
            pool.wait_ge(pv_filled, QUADS - T)
            fill_values(B - 1, T - 1)

        @block.scalar
        def _(act):
            def copy_keys(s, t, half):
                act.wait_ge(keys_filled, s * 2 + (half + 1))
                cols = slice(half * BANK, min((half + 1) * BANK, KEYS))
                act.activation(m.keys[:, t, cols], shared_r[:, 0:cols.stop - cols.start], ACT.Copy)\
                   .then_inc(keys_copied, 1)
                for g in range(G if half else 0):
                    rows = slice(ROWS * g, ROWS * g + SPLIT)
                    act.activation(plain[t % 2][rows, g, :], shared_r[rows, N:2 * N], ACT.Copy)\
                       .then_inc(plain_copied, 1)

            def copy_shifted(s, parity):
                act.wait_ge(shifted_filled, s + 1)
                for g in range(G):
                    rows = slice(ROWS * g, ROWS * (g + 1))
                    act.activation(shifted[parity][rows, g, :], shared_r[rows, 0:N], ACT.Copy)\
                       .then_inc(shifted_copied, 1)

            def step(g):
                b, r, s = g.b, g.r, g.s
                for u in range(UNITS):
                    if u == SHIFT_SLOT and g.maxes:
                        copy_shifted(s + 1, (r + 1) % 2)
                    if u == ATTN_SLOT and g.transpose_out:
                        act.wait_ge(attnT_filled, b + 1)
                        act.activation(attnT[:], shared_ps[:, 0:QT * P].rearrange("p (q n) -> p q n", n=P), ACT.Copy)\
                           .then_inc(attnT_copied, 1)
                    if u == KEYS_SLOT and g.transposes:
                        copy_keys(s + 3, (r + 3) % T, 0)
                    if u == QUERIES_SLOT and g.transposes:
                        copy_keys(s + 3, (r + 3) % T, 1)
                    if g.scores:
                        if u == 0:
                            wait_for(act, pv_filled, s - 1)
                        act.wait_ge(exp_filled, s * UNITS + (u + 1))
                        act.activation(probs[r % 2][:, u], exp_ps[u % 2][:].rearrange("p (g n) -> p g n", n=N),
                                       ACT.Exp).then_inc(exp_done, 1)
                    if u == 1 and g.output:
                        act.wait_ge(pv_filled, s)
                        wait_for(act, out_filled, s - 1)
                        act.activation(pv_sb[:], pv_ps[:, 0:N], ACT.Copy).then_inc(pv_copied, 1)

            act.wait_ge(blocks_zero, 4)
            for q in range(2):
                copy_keys(q, q, 0)
                copy_keys(q, q, 1)
            copy_shifted(0, 0)
            copy_keys(2, 2, 0)
            copy_keys(2, 2, 1)
            steps(act, step)

        @block.vector
        def _(vec):
            def reduce_unit(s, w, par):
                g, part = divmod(w, 3)
                vec.wait_ge(max_filled, s * MAXES + (w + 1))
                if part < 2:
                    out, bank = max_part[:, par, g, 0, part:part + 1], max_ps[w % 2][:]
                else:
                    out, bank = max_part[:, par, g, 1, :], max_ps[w % 2][:].rearrange("p (q n) -> p q n", n=N)
                vec.reduce_max(out, bank, axis=AX.X).then_inc(max_done, 1)

            def negate_max(s, t, par):
                slot = lambda n: m.query_rows[:, t, :, :, n].rearrange("p q g -> p g q")
                vec.wait_ge(max_done, s * MAXES + MAXES)
                vec.tensor_tensor(rowmax[:, par], max_part[:, par, :, 0], max_part[:, par, :, 1], ALU.max)\
                   .then_inc(chain, 1)
                vec.wait_ge(chain, s * 2 + 1)
                vec.tensor_scalar(slot(SPLIT), rowmax[:, par], -1.0, None, ALU.mult).then_inc(chain, 1)
                vec.wait_ge(chain, s * 2 + 2)
                vec.scalar_tensor_tensor(slot(SPLIT + 1), rowmax[:, par], -1.0, slot(SPLIT), ALU.mult, ALU.subtract)\
                   .then_inc(negmax_ready, 1)

            def normalize(g):
                t, par = (g.r - 1) % T, g.r % 2
                quad_out = shared_ps[:, 0:QT * P].rearrange("p (q g k) -> p q g k", q=QT, g=G)
                vec.wait_ge(out_filled, g.s)
                vec.reciprocal(rsum[:, par], quad_out[:, :, :, D:D + 1]).then_inc(rsum_ready, 1)
                vec.wait_ge(rsum_ready, g.s)
                if g.project:
                    vec.wait_ge(attnT_filled, g.b + 1)
                vec.tensor_tensor(attn[:, :, G * D * t:G * D * (t + 1)].rearrange("p q (g k) -> p q g k", g=G),
                                  quad_out[:, :, :, 0:D], rsum[:, par].to_broadcast([P, QT, G, D]), ALU.mult)\
                   .then_inc(out_done, 1)

            def step(g):
                b, r, s = g.b, g.r, g.s
                if g.maxes:
                    reduce_unit(s + 1, EARLY, (r + 1) % 2)
                if g.project:
                    vec.wait_ge(proj_filled, b + 1)
                    vec.tensor_tensor(m.x[:, bass.ts(b, QT), :],
                                      shared_ps[:, 0:QT * C].rearrange("p (q c) -> p q c", c=C),
                                      m.x[:, bass.ts(b, QT), :], ALU.add).then_inc(proj_done, 1)
                if g.maxes:
                    for w in range(EARLY + 1, MAXES):
                        reduce_unit(s + 1, w, (r + 1) % 2)
                    negate_max(s + 1, (r + 1) % T, (r + 1) % 2)
                for w in range(EARLY):
                    if g.early_maxes:
                        reduce_unit(s + 2, w, r % 2)
                    if w == EARLY // 3 and g.output:
                        normalize(g)

            for w in range(MAXES):
                reduce_unit(0, w, 0)
            negate_max(0, 0, 0)
            for w in range(EARLY):
                reduce_unit(1, w, 1)
            steps(vec, step)

        @block.tensor
        def _(pe):
            def transpose_rows(s, t, half):
                if half == 0:
                    pe.wait_ge(rows_ready, s * 3 + 3)
                else:
                    pe.wait_ge(keys_copied, s * 2 + 1)
                for k in range(4 * half, 4 * half + 4):
                    tile = m.key_rows[:, t, k] if k < KT else m.query_rows[:, t, k - KT]
                    mm = pe.transpose(shared_r[:, (k % 4) * P:(k % 4 + 1) * P],
                                      tile.rearrange("p g k -> p (g k)"), m.ident_r[:])
                mm.then_inc(keys_filled, 1)

            def max_unit(s, w, t, wait=True):
                g, part = divmod(w, 3)
                if w == 0:
                    pe.wait_ge(keys_copied, s * 2 + 2)
                    pe.wait_ge(plain_copied, s * G + G)
                if wait:
                    pe.wait_ge(max_done, s * MAXES + (w - 1))
                if part < 2:
                    mm = pe.matmul(max_ps[w % 2][:], plain[t % 2][:, g, part * P:(part + 1) * P],
                                   m.keys[:, t, 0:NC_], start=True, stop=True)
                else:
                    for q in range(QT):
                        mm = pe.matmul(max_ps[w % 2][:, q * N:(q + 1) * N],
                                       plain[t % 2][:, g, q * P:(q + 1) * P], m.keys[:, t, NC_:KEYS],
                                       start=True, stop=True)
                mm.then_inc(max_filled, 1)

            def shift_rows(s, t):
                pe.wait_ge(negmax_ready, s + 1)
                for q in range(QT):
                    mm = pe.transpose(shared_r[:, q * P:(q + 1) * P],
                                      m.query_rows[:, t, q].rearrange("p g k -> p (g k)"), m.ident_r[:])
                mm.then_inc(shifted_filled, 1)

            def exp_unit(s, u, t, par, wait=True):
                if u == 0:
                    pe.wait_ge(shifted_copied, s * G + G)
                if wait:
                    pe.wait_ge(exp_done, s * UNITS + (u - 1))
                for half in range(UNIT_BANKS):
                    mm = pe.matmul(exp_ps[u % 2][:, half * BANK:(half + 1) * BANK], m.keys[:, t, u * P:(u + 1) * P],
                                   shifted[par][:, 2 * half:2 * half + 2, :], start=True, stop=True)
                mm.then_inc(exp_filled, 1)

            def pv_tile(s, k, t, par):
                if k == 0:
                    pe.wait_ge(values_ready, s * 2 + 2)
                    wait_for(pe, pv_copied, s)
                pe.wait_ge(exp_done, s * UNITS + (k + 1))
                for g in range(G):
                    mm = pe.matmul(pv_ps[ROWS * g:ROWS * (g + 1), 0:N], m.value_cols[:, t, k, g, :],
                                   probs[par][:, k, g, :], start=(k == 0), stop=(k == KT - 1))
                if k == KT - 1:
                    mm.then_inc(pv_filled, 1)

            def step(g):
                b, r, s = g.b, g.r, g.s
                t, par = r % T, r % 2
                t1, t2 = (r + 1) % T, (r + 2) % T
                units = [(s + 1, w, t1) for w in range(EARLY, MAXES)] if g.maxes else []
                units += [(s + 2, w, t2) for w in range(EARLY)] if g.early_maxes else []

                def next_max():
                    if units:
                        max_unit(*units.pop(0))

                for u in range(UNITS):
                    next_max()
                    if u == 0 and g.project:
                        pe.wait_ge(attnT_copied, b + 1)
                        if g.early_maxes:
                            pe.wait_ge(plain_copied, s * G + 3 * G)
                        for q in range(QT):
                            mm = pe.matmul(shared_ps[:, q * C:(q + 1) * C], attnT[:, q, :], m.wproj[:],
                                           start=True, stop=True)
                        mm.then_inc(proj_filled, 1)
                    if u == SHIFT_SLOT and g.maxes:
                        if g.early_maxes:
                            pe.wait_ge(keys_copied, s * 2 + 6)
                            pe.wait_ge(plain_copied, s * G + 3 * G)
                        else:
                            pe.wait_ge(out_done, s - 1)
                        if g.project:
                            pe.wait_ge(proj_done, b + 1)
                        shift_rows(s + 1, t1)
                    if u == OUT_SLOT and g.output:
                        if g.maxes:
                            pe.wait_ge(shifted_copied, s * G + 2 * G)
                        else:
                            pe.wait_ge(out_done, s - 1)
                        pe.wait_ge(pv_copied, s)
                        for q in range(QT):
                            mm = pe.transpose(shared_ps[:, q * P:(q + 1) * P], pv_sb[:, q * P:(q + 1) * P], m.ident[:])
                        mm.then_inc(out_filled, 1)
                    if u == ATTN_SLOT and g.transpose_out:
                        pe.wait_ge(out_done, s)
                        for q in range(QT):
                            mm = pe.transpose(shared_ps[:, q * P:(q + 1) * P], attn[:, q, :], m.ident[:])
                        mm.then_inc(attnT_filled, 1)
                    if g.scores:
                        exp_unit(s, u, t, par, wait=r > 0 or u >= 2)
                    if u == KEYS_SLOT and g.transposes:
                        if g.output:
                            pe.wait_ge(out_done, s)
                        else:
                            pe.wait_ge(shifted_copied, s * G + 2 * G)
                        if g.transpose_out:
                            pe.wait_ge(attnT_copied, b + 1)
                        transpose_rows(s + 3, (r + 3) % T, 0)
                    if u == QUERIES_SLOT and g.transposes:
                        transpose_rows(s + 3, (r + 3) % T, 1)
                    next_max()
                    if g.output:
                        for k in PV_BEFORE[u]:
                            pv_tile(s - 1, k, (r - 1) % T, 1 - par)
                    if g.scores:
                        for k in PV_NOW[u]:
                            pv_tile(s, k, t, par)

            transpose_rows(0, 0, 0)
            transpose_rows(0, 0, 1)
            for q in range(1, 2):
                pe.wait_ge(keys_copied, 2)
                pe.wait_ge(plain_copied, G)
                transpose_rows(q, q, 0)
                transpose_rows(q, q, 1)
            for w in range(MAXES):
                max_unit(0, w, 0, wait=w >= 2)
            pe.wait_ge(keys_copied, 4)
            pe.wait_ge(plain_copied, 2 * G)
            shift_rows(0, 0)
            pe.wait_ge(shifted_copied, G)
            transpose_rows(2, 2, 0)
            transpose_rows(2, 2, 1)
            for w in range(EARLY):
                max_unit(1, w, 1)
            steps(pe, step)


class Memory:

    def __init__(self, nc, ctx):
        sb = lambda name, shape, dt=F32: ctx.enter_context(nc.sbuf_tensor(name, shape, dt))
        self.x = sb("x", [P, TILES, C])
        self.gate, self.up = sb("gate", [P, E, I]), sb("up", [P, E, I])
        self.ones = sb("ones", [P, P])
        self.eps = sb("eps_sb", [P, 1])
        self.ident = sb("ident", [P, P])
        self.gate_up_in = ctx.enter_context(nc.semaphore("gate_up_in"))

    def for_attention(self, nc, ctx):
        sb = lambda name, shape, dt=F32: ctx.enter_context(nc.sbuf_tensor(name, shape, dt))
        self.context = sb("context", [P, B * CT, 2 * C])
        self.qkv = sb("qkv", [P, TILES, 3 * C])
        self.key_rows = sb("key_rows", [P, T, KT, G, ROWS], F32R)
        self.query_rows = sb("query_rows", [P, T, QT, G, ROWS], F32R)
        self.value_cols = sb("value_cols", [P, T, KT, G, ROWS])
        self.keys = sb("keys", [P, T, KEYS], F32R)
        self.wproj = sb("wproj", [P, C])
        self.bproj = sb("bproj", [1, C])
        self.bias = sb("bias", [P, C])
        self.ident_r = sb("ident_r", [P, P], F32R)
        self.context_in = [ctx.enter_context(nc.semaphore(f"context_in{b}")) for b in range(B)]


def build(nc, d, out):
    with ExitStack() as ctx:
        m = Memory(nc, ctx)
        with ExitStack() as attention:
            m.for_attention(nc, attention)
            project(nc, m, d)
            attend(nc, m, d)
        experts(nc, m, d, out)


SLOTS = (2 * TILES * P + E * (P - 1)) // P
SLOTS_PAD = -(-SLOTS // 4) * 4
PICKS = 2 * TILES * P
VECTOR_SLOTS = 5 * TILES // 4
CHUNKS = 4


def experts(nc, m, d, out):
    with ExitStack() as ctx:
        sem = lambda name: ctx.enter_context(nc.semaphore(name))
        sb = lambda name, shape, dt=F32: ctx.enter_context(nc.sbuf_tensor(name, shape, dt))
        psum = lambda name: ctx.enter_context(nc.psum_tensor(name, [P, BANK], F32))
        ln = [sem(n) for n in ("ln2_stats", "ln2_aggr", "ln2_std", "ln2_rstd", "ln2_norm")]
        router_in, down_in, const_start, const_ready = sem("router_in"), sem("down_in"), sem("const_start"), sem("const_ready")
        ht_filled, ht_copied = sem("ht_filled"), sem("ht_copied")
        const_filled, const_copied = sem("const_filled"), sem("const_copied")
        logits_filled, logits_done, conf_done = sem("logits_filled"), sem("logits_done"), sem("conf_done")
        gap_ready, weights_done = sem("gap_ready"), sem("weights_done")
        route = sem("route")
        picks_ready, place_filled, table_ready = sem("picks_ready"), sem("place_filled"), sem("table_ready")
        mask_ready = sem("mask_ready")
        h_stored, count_consts = sem("h_stored"), sem("count_consts")
        lanes_ready, one_lane, one_slot = sem("lanes_ready"), sem("one_lane"), sem("one_slot")
        late_slot = sem("late_slot")
        picks_found, sources_ready = sem("picks_found"), sem("sources_ready")
        source_copied, target_copied = sem("source_copied"), sem("target_copied")
        y_loaded = [sem(f"y_loaded{i}") for i in range(CHUNKS)]
        x_loaded = [sem(f"x_loaded{i}") for i in range(4)]
        y_stored = [sem(f"y_stored{i}") for i in range(4)]
        xT_filled, xT_copied = sem("xT_filled"), sem("xT_copied")
        gate_filled, up_filled = sem("gate_filled"), sem("up_filled")
        silu_done, act_done = sem("silu_done"), sem("act_done")
        actT_filled, actT_copied = sem("actT_filled"), sem("actT_copied")
        y_filled, y_copied = sem("y_filled"), sem("y_copied")
        summed, stored = sem("summed"), sem("stored")

        h_dram = nc.dram_tensor("h_rows", (TILES * P, C), F32, kind="Internal").ap()
        outs_dram = nc.dram_tensor("pick_outs", (PICKS + SLOTS_PAD * P, C), F32, kind="Internal").ap()
        stats, aggr, rstd = sb("ln2_stats_sb", [P, TILES, 6]), sb("ln2_aggr_sb", [P, TILES, 2]), sb("ln2_rstd_sb", [P, 2, TILES])
        h = sb("h", [P, TILES, C])
        hT = sb("hT", [P, TILES * P])
        down = sb("down", [P, E, IC, C])
        conf_w = sb("conf_w", [P, E])
        conf_rows = sb("conf_rows", [1, 2 * E])
        conf_all = sb("conf_all", [P, 2, E])
        earlier = sb("earlier", [P, E, E])
        before = sb("before", [P, P])
        before_r, ones_r = sb("before_r", [P, P], F32R), sb("ones_r", [P, P], F32R)
        lane_index = sb("lane_index", [P, P])
        slot_of = sb("slot_of", [P, SLOTS_PAD])
        pick_id = sb("pick_id", [P, 2 * TILES])
        spare_id = sb("spare_id", [P, SLOTS_PAD])
        lane_i, slot_i = sb("lane_i", [P, 2 * TILES], I32), sb("slot_i", [P, 2 * TILES], I32)
        lane, slot = sb("lane", [P, 2 * TILES]), sb("slot", [P, 2 * TILES])
        lane_hot = sb("lane_hot", [P, 2 * TILES, P], F32R)
        slot_hot = sb("slot_hot", [P, 2 * TILES, SLOTS_PAD], F32R)
        found, second, token = sb("found", [P, SLOTS_PAD]), sb("second", [P, SLOTS_PAD]), sb("token", [P, SLOTS_PAD])
        spare = sb("spare", [P, SLOTS_PAD])
        source = sb("source", [P, SLOTS_PAD], mybir.dt.uint32)
        target = sb("target", [P, SLOTS_PAD], mybir.dt.uint32)
        tile_start = sb("tile_start", [P, E, TILES])
        slot_index = sb("slot_index", [1, SLOTS_PAD, E])
        z, bids = sb("z", [P, TILES, E]), sb("bids", [P, TILES, E])
        pair, pair2 = sb("pair", [P, TILES, E, E]), sb("pair2", [P, TILES, E, E])
        rank = sb("rank", [P, TILES, E])
        top = sb("top", [P, 2, TILES, E])
        picked = sb("picked", [P, 2, TILES, E])
        best = sb("best", [P, 2, TILES, 1])
        gap, weight = sb("gap", [P, 2, TILES, 1]), sb("weight", [P, 2, TILES, 1])
        picks = sb("picks", [P, TILES + 1, E], F32R)
        place = sb("place", [P, TILES, E])
        row_f, row = sb("row_f", [P, 2, TILES]), sb("row", [P, 2 * TILES], I32)
        count, full = sb("count", [P, E]), sb("full", [P, E, TILES])
        tiles_of, first, end = sb("tiles_of", [P, E]), sb("first_slot", [P, E]), sb("end_slot", [P, E])
        before_e = sb("before_e", [P, E, E])
        ended, slot_e = sb("ended", [1, SLOTS_PAD, E]), sb("slot_e", [1, SLOTS_PAD])
        table = sb("table", [1, SLOTS_PAD], I32)
        source_now = sb("source_now", [P, 4], mybir.dt.uint32)
        target_now = sb("target_now", [P, 4], mybir.dt.uint32)
        x_in = sb("x_in", [P, 4, C])
        xT = sb("xT", [P, 2, P])
        silu, hidden = sb("silu", [P, 2, I]), sb("hidden", [P, 2, I])
        hiddenT = sb("hiddenT", [P, 2, IC, P])
        y_out = sb("y_out", [P, 4, C])
        y_in = sb("y_in", [P, 2, TILES, C])
        t_ps = [psum(f"t_ps{i}") for i in range(2)]
        gate_ps, up_ps = [psum(f"gate_ps{i}") for i in range(2)], [psum(f"up_ps{i}") for i in range(2)]
        at_ps = [psum(f"at_ps{i}") for i in range(2)]
        xT_ps, y_ps = t_ps
        CONSTS = 8
        block = ctx.enter_context(nc.Block())

        def slots(engine, step, last):
            for j in range(8):
                step(*divmod(j, 4))
            with engine.Fori(2, SLOTS_PAD // 4 - 1) as i:
                for r in range(4):
                    step(i, r)
            for r in range(last - (SLOTS_PAD - 4)):
                step(SLOTS_PAD // 4 - 1, r)

        def exists(i, r, shift):
            return not isinstance(i, int) or 0 <= 4 * i + r + shift < SLOTS_PAD

        def hot_slot(engine, k):
            return engine.tensor_scalar(slot_hot[:, k, :], slot_of[:], slot[:, k:k + 1], pick_id[:, k:k + 1],
                                        ALU.is_equal, ALU.mult)

        @block.sync
        def _(sp):
            sp.dma_start(conf_w[:], d["conf_wT"]).then_inc(router_in, 16)
            sp.dma_start(conf_rows[:, 0:E], d["conf_b"].rearrange("(a e) -> a e", a=1)).then_inc(router_in, 16)
            sp.dma_start(conf_rows[:, E:2 * E], d["wealth"].rearrange("(a e) -> a e", a=1)).then_inc(router_in, 16)
            sp.dma_start(down[:], d["downT"].rearrange("e (c p) h -> p e c h", p=P)).then_inc(down_in, 16)
            for k in range(4):
                sp.wait_ge(ln[4], (k + 1) * 4)
                sp.dma_start(h_dram[k * 4 * P:(k + 1) * 4 * P, :].rearrange("(t p) c -> p t c", p=P),
                             h[:, k * 4:(k + 1) * 4, :]).then_inc(h_stored, 16)
            for r in range(4):
                sp.wait_ge(y_stored[r], 16 * (SLOTS_PAD // 4))
            for c in range(CHUNKS):
                for k in range(2):
                    n = TILES // CHUNKS
                    first_row = (k * TILES + c * n) * P
                    sp.dma_start(y_in[:, k, c * n:(c + 1) * n, :],
                                 outs_dram[first_row:first_row + n * P, :].rearrange("(t p) c -> p t c", p=P))\
                      .then_inc(y_loaded[c], 16)

        @block.gpsimd
        def _(pool):
            iota = lambda out, pattern, base, per_partition: pool.iota(
                out, pattern=pattern, base=base, channel_multiplier=per_partition,
                allow_small_or_imprecise_dtypes=True).then_inc(const_ready, 1)
            pool.memset(earlier[:], 1.0).then_inc(const_start, 1)
            pool.memset(before[:], 1.0).then_inc(const_start, 1)
            iota(tile_start[:], [[0, E], [P, TILES]], 0, 0)
            iota(slot_index[:], [[1, SLOTS_PAD], [0, E]], 0, 0)
            iota(lane_index[:], [[1, P]], 0, 0)
            iota(slot_of[:], [[1, SLOTS_PAD]], 0, 0)
            iota(pick_id[:], [[P, 2 * TILES]], 1, 1)
            iota(spare_id[:], [[P, SLOTS_PAD]], PICKS + 1, 1)
            pool.memset(picks[:, TILES, :].bitcast(F32), 0.0).then_inc(const_ready, 1)
            pool.memset(ones_r[:].bitcast(F32), 1.0).then_inc(const_ready, 1)
            pool.wait_ge(const_start, 2)
            pool.affine_select(out=earlier[:], in_=earlier[:], compare_op=ALU.is_gt, fill=0.0, base=0,
                               pattern=[[1, E], [-1, E]], channel_multiplier=0).then_inc(mask_ready, 1)
            pool.affine_select(out=before[:], in_=before[:], compare_op=ALU.is_gt, fill=0.0, base=0,
                               pattern=[[1, P]], channel_multiplier=-1).then_inc(mask_ready, 1)
            pool.wait_ge(mask_ready, 2)
            pool.tensor_copy(before_r[:], before[:]).then_inc(count_consts, 1)
            pool.wait_ge(const_ready, CONSTS)
            pool.wait_ge(lanes_ready, 2)
            for k in range(VECTOR_SLOTS, 2 * TILES):
                hot_slot(pool, k).then_inc(late_slot, 1)
            pool.wait_ge(h_stored, 64)
            pool.wait_ge(sources_ready, 2)

            def load(r):
                pool.indirect_dma_start(x_in[:, r, :], None, h_dram,
                                        bass.IndirectOffsetOnAxis(ap=source_now[:, r:r + 1], axis=0))\
                    .then_inc(x_loaded[r], 16)

            def step(i, r):
                j = 4 * i + r
                before2, before1 = (r - 2) % 4, (r - 1) % 4
                if exists(i, r, 3):
                    pool.wait_ge(xT_filled, j + 1)
                    pool.wait_ge(source_copied, j + 4)
                if exists(i, r, -2):
                    pool.wait_ge(y_copied, j - 1)
                    pool.wait_ge(target_copied, j - 1)
                if exists(i, r, -5):
                    pool.wait_ge(y_stored[before1], (i + (r - 5) // 4 + 1) * 16)
                if exists(i, r, 4):
                    pool.tensor_copy(source_now[:, r:r + 1], source[:, bass.ds(j + 4, 1)]).then_inc(source_copied, 1)
                if exists(i, r, -1):
                    pool.tensor_copy(target_now[:, before1:before1 + 1], target[:, bass.ds(j - 1, 1)])\
                        .then_inc(target_copied, 1)
                if exists(i, r, 3):
                    load((r + 3) % 4)
                if exists(i, r, -2):
                    pool.indirect_dma_start(outs_dram,
                                            bass.IndirectOffsetOnAxis(ap=target_now[:, before2:before2 + 1], axis=0),
                                            y_out[:, before2, :], None).then_inc(y_stored[before2], 16)

            for r in range(4):
                pool.tensor_copy(source_now[:, r:r + 1], source[:, r:r + 1]).then_inc(source_copied, 1)
            pool.wait_ge(source_copied, 3)
            for r in range(3):
                load(r)
            slots(pool, step, SLOTS_PAD + 2)

        @block.scalar
        def _(act):
            _, scalar_std, _ = layernorm(None, act, m.x, h, stats, aggr, rstd, ln)
            scalar_std(m.eps[:])
            for k in range(4):
                act.wait_ge(ht_filled, k + 1)
                act.activation(hT[:, k * BANK:(k + 1) * BANK], t_ps[k % 2][:], ACT.Copy).then_inc(ht_copied, 1)
            act.wait_ge(logits_done, 1)
            act.activation(bids[:], z[:], ACT.Sigmoid).then_inc(conf_done, 1)
            act.wait_ge(gap_ready, 2)
            act.activation(weight[:], gap[:], ACT.Sigmoid).then_inc(weights_done, 1)

            def step(i, r):
                j = 4 * i + r
                if exists(i, r, 0):
                    act.wait_ge(gate_filled, j + 1)
                    wait_for(act, act_done, j - 1)
                    act.activation(silu[:, r % 2, :], gate_ps[r % 2][:], ACT.Silu).then_inc(silu_done, 1)
                if exists(i, r, -1):
                    act.wait_ge(actT_filled, j)
                    wait_for(act, y_filled, j - 2)
                    act.activation(hiddenT[:, (r - 1) % 2], at_ps[(r - 1) % 2][:].rearrange("p (c n) -> p c n", n=P),
                                   ACT.Copy).then_inc(actT_copied, 1)

            slots(act, step, SLOTS_PAD + 1)
            n = TILES // CHUNKS
            for c in range(CHUNKS):
                act.wait_ge(summed, 2 * n * (c + 1))
                act.dma_start(out.rearrange("b (t p) c -> p (b t) c", p=P)[:, c * n:(c + 1) * n, :],
                              m.x[:, c * n:(c + 1) * n, :]).then_inc(stored, 16)
            act.wait_ge(stored, 16 * CHUNKS)

        @block.vector
        def _(vec):
            vector_stats, _, vector_norm = layernorm(vec, None, m.x, h, stats, aggr, rstd, ln)
            vector_stats()
            for i in range(TILES):
                vector_norm(i, first=i == 0)
            vec.wait_ge(const_filled, 1)
            vec.tensor_copy(conf_all[:], up_ps[0][:, 0:2 * E].rearrange("p (k e) -> p k e", e=E)).then_inc(const_copied, 1)
            vec.wait_ge(const_copied, 1)
            vec.wait_ge(logits_filled, 1)
            over_tiles = lambda ap: ap.unsqueeze(1).to_broadcast([P, TILES, E])
            vec.tensor_tensor(z[:], up_ps[1][:, 0:TILES * E].rearrange("p (t e) -> p t e", e=E),
                              over_tiles(conf_all[:, 0, :]), ALU.add).then_inc(logits_done, 1)
            steps = [0]

            def then(op):
                steps[0] += 1
                op.then_inc(route, 1)
                vec.wait_ge(route, steps[0])

            vec.wait_ge(conf_done, 1)
            then(vec.tensor_tensor(bids[:], bids[:], over_tiles(conf_all[:, 1, :]), ALU.mult))
            pairs = [P, TILES, E, E]
            this, other = bids[:].unsqueeze(3).to_broadcast(pairs), bids[:].unsqueeze(2).to_broadcast(pairs)
            vec.wait_ge(mask_ready, 2)
            vec.wait_ge(const_ready, CONSTS)
            vec.tensor_tensor(pair2[:], other, this, ALU.is_gt)
            then(vec.tensor_tensor(pair[:], other, this, ALU.is_equal))
            then(vec.tensor_tensor(pair[:], pair[:], earlier[:].unsqueeze(1).to_broadcast(pairs), ALU.mult))
            then(vec.tensor_tensor(pair[:], pair[:], pair2[:], ALU.add))
            then(vec.tensor_reduce(rank[:], pair[:], axis=AX.X, op=ALU.add))
            vec.tensor_scalar(picks[:, 0:TILES, :], rank[:], 1.5, None, ALU.is_lt).then_inc(picks_ready, 1)
            for k in range(2):
                op = vec.tensor_scalar(top[:, k], rank[:], float(k), None, ALU.is_equal)
            then(op)
            for k in range(2):
                op = vec.tensor_tensor(picked[:, k], top[:, k], bids[:], ALU.mult)
            then(op)
            then(vec.tensor_reduce(best[:, :, :, 0], picked[:], axis=AX.X, op=ALU.add))
            for k in range(2):
                vec.tensor_tensor(gap[:, k], best[:, k], best[:, 1 - k], ALU.subtract).then_inc(gap_ready, 1)
            vec.wait_ge(place_filled, 1)
            then(vec.tensor_copy(count[:], t_ps[0][:, TILES * E:(TILES + 1) * E]))
            then(vec.tensor_tensor(full[:], count[:].unsqueeze(2).to_broadcast([P, E, TILES]), tile_start[:], ALU.is_gt))
            then(vec.tensor_reduce(tiles_of[:], full[:], axis=AX.X, op=ALU.add))
            then(vec.tensor_tensor(before_e[:], earlier[:], tiles_of[:].unsqueeze(1).to_broadcast([P, E, E]), ALU.mult))
            then(vec.tensor_reduce(first[:], before_e[:], axis=AX.X, op=ALU.add))
            then(vec.scalar_tensor_tensor(place[:], over_tiles(first[:]), float(P),
                                          t_ps[0][:, 0:TILES * E].rearrange("p (t e) -> p t e", e=E),
                                          ALU.mult, ALU.add))
            for k in range(2):
                op = vec.tensor_tensor(picked[:, k], top[:, k], place[:], ALU.mult)
            then(op)
            then(vec.tensor_reduce(row_f[:], picked[:], axis=AX.X, op=ALU.add))
            then(vec.tensor_copy(row[:], row_f[:].rearrange("p k t -> p (k t)")))
            vec.tensor_scalar(lane_i[:], row[:], P - 1, None, ALU.bitwise_and)
            then(vec.tensor_scalar(slot_i[:], row[:], P.bit_length() - 1, None, ALU.logical_shift_right))
            vec.tensor_copy(slot[:], slot_i[:]).then_inc(lanes_ready, 1)
            vec.tensor_copy(lane[:], lane_i[:]).then_inc(lanes_ready, 1)
            vec.wait_ge(lanes_ready, 2)
            for k in range(2 * TILES):
                vec.tensor_scalar(lane_hot[:, k, :], lane_index[:], lane[:, k:k + 1], None, ALU.is_equal)\
                   .then_inc(one_lane, 1)
                if k < VECTOR_SLOTS:
                    hot_slot(vec, k).then_inc(one_slot, 1)
            then(vec.tensor_tensor(end[:], first[:], tiles_of[:], ALU.add))
            then(vec.tensor_tensor(ended[:], slot_index[:], end[0:1].unsqueeze(1).to_broadcast([1, SLOTS_PAD, E]), ALU.is_ge))
            then(vec.tensor_reduce(slot_e[:], ended[:, :, 0:E - 1], axis=AX.X, op=ALU.add))
            vec.tensor_copy(table[:], slot_e[:]).then_inc(table_ready, 1)
            vec.wait_ge(picks_found, 1)
            then(vec.tensor_copy(found[:], gate_ps[0][:, 0:SLOTS_PAD]))
            vec.scalar_tensor_tensor(spare[:], found[:], 0.0, spare_id[:], ALU.is_equal, ALU.mult)
            then(vec.tensor_scalar(second[:], found[:], float(TILES * P) + 0.5, float(TILES * P), ALU.is_gt, ALU.mult))
            vec.scalar_tensor_tensor(target[:], spare[:], -1.0, found[:], ALU.add, ALU.add).then_inc(sources_ready, 1)
            then(vec.tensor_tensor(token[:], found[:], second[:], ALU.subtract))
            vec.tensor_scalar(source[:], token[:], -1.0, 0.0, ALU.add, ALU.max).then_inc(sources_ready, 1)

            def copy_xT(j, r):
                vec.wait_ge(xT_filled, j + 1)
                wait_for(vec, up_filled, j - 1)
                vec.tensor_copy(xT[:, r % 2, :], xT_ps[:, 0:P]).then_inc(xT_copied, 1)

            def step(i, r):
                j = 4 * i + r
                if exists(i, r, 0):
                    vec.wait_ge(silu_done, j + 1)
                    vec.wait_ge(up_filled, j + 1)
                    wait_for(vec, actT_filled, j - 1)
                    vec.tensor_tensor(hidden[:, r % 2, :], up_ps[r % 2][:], silu[:, r % 2, :], ALU.mult)\
                       .then_inc(act_done, 1)
                if exists(i, r, 1):
                    copy_xT(j + 1, r + 1)
                if exists(i, r, -2):
                    vec.wait_ge(y_filled, j - 1)
                    if not isinstance(i, int) or j >= 6:
                        vec.wait_ge(y_stored[(r - 2) % 4], (i if r >= 2 else i - 1) * 16)
                    vec.tensor_copy(y_out[:, (r - 2) % 4, :], y_ps[:, 0:C]).then_inc(y_copied, 1)

            copy_xT(0, 0)
            slots(vec, step, SLOTS_PAD + 2)
            for t in range(TILES):
                if t % (TILES // CHUNKS) == 0:
                    vec.wait_ge(y_loaded[t // (TILES // CHUNKS)], 32)
                if t == 0:
                    vec.wait_ge(weights_done, 1)
                for k in range(2):
                    if k:
                        vec.wait_ge(summed, 2 * t + 1)
                    vec.scalar_tensor_tensor(m.x[:, t, :], y_in[:, k, t, :], weight[:, k, t, :], m.x[:, t, :],
                                             ALU.mult, ALU.add).then_inc(summed, 1)

        @block.tensor
        def _(pe):
            def logits(k):
                for i in range(4 * k, 4 * k + 4):
                    mm = pe.matmul(up_ps[1][:, i * E:(i + 1) * E], hT[:, i * P:(i + 1) * P], conf_w[:], start=True, stop=True)
                return mm

            pe.wait_ge(router_in, 48)
            pe.matmul(up_ps[0][:, 0:2 * E], m.ones[0:1, :], conf_rows[0:1, :], start=True, stop=True)\
              .then_inc(const_filled, 1)
            for k in range(4):
                pe.wait_ge(ln[4], (k + 1) * 4)
                if k >= 2:
                    pe.wait_ge(ht_copied, k - 1)
                for i in range(4):
                    mm = pe.transpose(t_ps[k % 2][:, i * P:(i + 1) * P], h[:, k * 4 + i, :], m.ident[:])
                mm.then_inc(ht_filled, 1)
                if k >= 2:
                    logits(k - 2)
            pe.wait_ge(ht_copied, 3)
            logits(2)
            pe.wait_ge(ht_copied, 4)
            logits(3).then_inc(logits_filled, 1)
            pe.wait_ge(picks_ready, 1)
            pe.wait_ge(count_consts, 1)
            pe.wait_ge(const_ready, CONSTS)
            pe.matmul(t_ps[0][:, 0:(TILES + 1) * E], before_r[:], picks[:].rearrange("p t e -> p (t e)"),
                      start=True, stop=False)
            for t in range(TILES):
                n = TILES - t
                mm = pe.matmul(t_ps[0][:, (t + 1) * E:(TILES + 1) * E], ones_r[:],
                               picks[:, t, :].unsqueeze(1).to_broadcast([P, n, E]), start=False, stop=(t == TILES - 1))
            mm.then_inc(place_filled, 1)
            for k in range(2 * TILES):
                pe.wait_ge(one_lane, k + 1)
                if k < VECTOR_SLOTS:
                    pe.wait_ge(one_slot, k + 1)
                else:
                    pe.wait_ge(late_slot, k + 1 - VECTOR_SLOTS)
                mm = pe.matmul(gate_ps[0][:, 0:SLOTS_PAD], lane_hot[:, k, :], slot_hot[:, k, :],
                               start=(k == 0), stop=(k == 2 * TILES - 1))
            mm.then_inc(picks_found, 1)
            pe.wait_ge(sources_ready, 2)
            pe.wait_ge(m.gate_up_in, 32)
            pe.wait_ge(down_in, 16)
            pe.wait_ge(table_ready, 1)

            def expert(j):
                return pe.value_load(table[0:1, bass.ds(j, 1)], min_val=0, max_val=E - 1)

            def transpose_x(i, r, shift):
                j, r4 = 4 * i + r + shift, (r + shift) % 4
                pe.wait_ge(x_loaded[r4], (i + (r + shift) // 4) * 16 + 16)
                wait_for(pe, xT_copied, j)
                pe.transpose(xT_ps[:, 0:P], x_in[:, r4, :], m.ident[:]).then_inc(xT_filled, 1)

            def step(i, r):
                j = 4 * i + r
                if exists(i, r, 0):
                    e = expert(j)
                    pe.wait_ge(xT_copied, j + 1)
                    wait_for(pe, silu_done, j - 1)
                    pe.matmul(gate_ps[r % 2][:], xT[:, r % 2, :], m.gate[:, bass.ds(e, 1), :].rearrange("p a i -> p (a i)"),
                              start=True, stop=True).then_inc(gate_filled, 1)
                    wait_for(pe, act_done, j - 1)
                    pe.matmul(up_ps[r % 2][:], xT[:, r % 2, :], m.up[:, bass.ds(e, 1), :].rearrange("p a i -> p (a i)"),
                              start=True, stop=True).then_inc(up_filled, 1)
                if exists(i, r, 1):
                    transpose_x(i, r, 1)
                if exists(i, r, -2):
                    e = expert(j - 2)
                    pe.wait_ge(actT_copied, j - 1)
                    wait_for(pe, y_copied, j - 2)
                    for c in range(IC):
                        mm = pe.matmul(y_ps[:, 0:C], hiddenT[:, r % 2, c, :],
                                       down[:, bass.ds(e, 1), c, :].rearrange("p a h -> p (a h)"),
                                       start=(c == 0), stop=(c == IC - 1))
                    mm.then_inc(y_filled, 1)
                if exists(i, r, -1):
                    pe.wait_ge(act_done, j)
                    wait_for(pe, actT_copied, j - 2)
                    for c in range(IC):
                        mm = pe.transpose(at_ps[(r - 1) % 2][:, c * P:(c + 1) * P],
                                          hidden[:, (r - 1) % 2, c * P:(c + 1) * P], m.ident[:])
                    mm.then_inc(actT_filled, 1)

            transpose_x(0, 0, 0)
            slots(pe, step, SLOTS_PAD + 2)


def kernel(x, ctx_2048, L0_xattn_w_qkv, L0_xattn_w_proj, L0_xattn_b_proj, L0_ffn_conf_w, L0_ffn_conf_b,
           L0_ffn_gate_w, L0_ffn_up_w, L0_ffn_down_w, L0_ffn_wealth):
    import concourse.bacc as bacc
    from concourse.bass_utils import run_bass_kernel_spmd

    t = lambda a: np.ascontiguousarray(np.swapaxes(np.asarray(a), -1, -2))
    arrays = {
        "x": np.asarray(x), "ctx": np.asarray(ctx_2048), "w_qkvT": t(L0_xattn_w_qkv),
        "w_projT": t(L0_xattn_w_proj), "b_proj": np.asarray(L0_xattn_b_proj),
        "conf_wT": t(L0_ffn_conf_w), "conf_b": np.asarray(L0_ffn_conf_b), "wealth": np.asarray(L0_ffn_wealth),
        "gateT": t(L0_ffn_gate_w), "upT": t(L0_ffn_up_w), "downT": t(L0_ffn_down_w),
    }
    nc = bacc.Bacc("TRN2", target_bir_lowering=False, num_devices=1)
    d = {k: nc.dram_tensor(f"{k}_dram", a.shape, mybir.dt.from_np(a.dtype), kind="ExternalInput").ap() for k, a in arrays.items()}
    out = nc.dram_tensor("out_dram", (B, N, C), F32, kind="ExternalOutput").ap()
    build(nc, d, out)
    r = run_bass_kernel_spmd(nc, [{f"{k}_dram": a for k, a in arrays.items()}], core_ids=[0])
    return r.results[0]["out_dram"]
```
